# Optimizing a Trainium2 kernel written in Bass

```python
import numpy as np
import jax
import jax.numpy as jnp

def _softmax(x, axis=-1):
    return jax.nn.softmax(x, axis=axis)

def _gelu(x):
    return jax.nn.gelu(x, approximate=True)

def _silu(x):
    return jax.nn.silu(x)

def _sigmoid(x):
    return jax.nn.sigmoid(x)

def _layernorm(x, axis=-1, eps=1e-05):
    m = jnp.mean(x, axis=axis, keepdims=True)
    v = jnp.var(x, axis=axis, keepdims=True)
    return (x - m) / jnp.sqrt(v + eps)

def _scatter_add(tgt, idx, src, axis=0):
    return tgt.at[idx].add(src)

def _segment_sum(src, seg, n):
    return jax.ops.segment_sum(src, seg, n)
kernel_name = 'mk_cond_resid_d2_seqx_r4_dc1de0'

def setup_inputs(seed: int=0):
    np.random.seed(seed)
    _w = jnp.asarray

    def _rec_inputs():
        import jax
        import jax.numpy as jnp
        _rk = jax.random.key(seed)
        x = -0.0002928 + 1 * jax.random.normal(jax.random.fold_in(_rk, 1), (16, 256, 256), jnp.float32)
        _lenS = 256 - jax.random.randint(jax.random.fold_in(_rk, 7), (16,), 0, max(1, 256 // 4) + 1, jnp.int32)
        _lenS2 = 256 - jax.random.randint(jax.random.fold_in(_rk, 8), (16,), 0, max(1, 256 // 4) + 1, jnp.int32)
        cond_64 = -0.0184271 + 1.00439 * jax.random.normal(jax.random.fold_in(_rk, 12), (16, 64), jnp.float32)
        _validS = jnp.arange(256)[None, :] < _lenS[:, None]
        _validS2 = jnp.arange(256)[None, :] < _lenS2[:, None]
        _causal = jnp.tril(jnp.ones((256, 256), dtype=bool))
        mask_BxS_bf1 = jnp.ones((16, 256), dtype=bool)
        return (x, cond_64, mask_BxS_bf1)
    x, cond_64, mask_BxS_bf1 = _rec_inputs()

    def _L0_cond_setup():
        import jax, jax.numpy as jnp
        import numpy as np
        DIM = 256
        HEADS = 16
        DIM_HEAD = 64
        SCALE = 8.0

        def ln(x, g, eps=1e-05):
            mean = x.mean(axis=-1, keepdims=True)
            var = ((x - mean) ** 2).mean(axis=-1, keepdims=True)
            return (x - mean) * jax.lax.rsqrt(var + eps) * g

        def l2norm(t):
            n = jnp.maximum(jnp.linalg.norm(t, axis=-1, keepdims=True), 1e-12)
            return t / n

        def rel_pos_bias(n, w0, b0, g0, w1, b1, g1, w2, b2, dtype):
            pos = jnp.arange(-n + 1, n, dtype=dtype)[:, None]
            h = jax.nn.silu(ln(pos @ w0 + b0, g0))
            h = jax.nn.silu(ln(h @ w1 + b1, g1))
            h = h @ w2 + b2
            i = jnp.arange(n)
            idx = i[:, None] - i[None, :] + n - 1
            bias = h[idx]
            return jnp.transpose(bias, (2, 0, 1))
        key = jax.random.key(seed)
        ks = jax.random.split(key, 16)
        b, n = (2, 512)
        inner = HEADS * DIM_HEAD
        s = 0.02
        return {'x': jax.random.normal(ks[0], (b, n, DIM), jnp.float32), 'mask': jnp.ones((b, n), dtype=bool), 'g_norm': jnp.ones((DIM,), jnp.float32), 'Wq': jax.random.normal(ks[1], (DIM, inner), jnp.float32) * s, 'Wkv': jax.random.normal(ks[2], (DIM, 2 * DIM_HEAD), jnp.float32) * s, 'q_scale': jnp.ones((DIM_HEAD,), jnp.float32), 'k_scale': jnp.ones((DIM_HEAD,), jnp.float32), 'null_kv': jax.random.normal(ks[3], (2, DIM_HEAD), jnp.float32), 'null_attn_bias': jax.random.normal(ks[4], (HEADS,), jnp.float32), 'w0': jax.random.normal(ks[5], (1, DIM), jnp.float32) * s, 'b0': jnp.zeros((DIM,), jnp.float32), 'g0': jnp.ones((DIM,), jnp.float32), 'w1': jax.random.normal(ks[6], (DIM, DIM), jnp.float32) * s, 'b1': jnp.zeros((DIM,), jnp.float32), 'g1': jnp.ones((DIM,), jnp.float32), 'w2': jax.random.normal(ks[7], (DIM, HEADS), jnp.float32) * s, 'b2': jnp.zeros((HEADS,), jnp.float32), 'Wout': jax.random.normal(ks[8], (inner, DIM), jnp.float32) * s, 'g_out': jnp.ones((DIM,), jnp.float32)}
    _L0_cond_all = _L0_cond_setup()
    _L0_cond_in = {k: v for k, v in _L0_cond_all.items() if k in ('g_norm', 'Wq', 'Wkv', 'q_scale', 'k_scale', 'null_attn_bias', 'w0', 'b0', 'g0', 'w1', 'b1', 'g1', 'w2', 'b2', 'Wout', 'g_out')}
    del _L0_cond_all

    def _L1_cond_setup():
        import jax, jax.numpy as jnp
        import numpy as np
        B, S, H = (4, 512, 256)
        E = 8
        M = 128
        K = 2
        N_SHARED = 2
        SM = M * N_SHARED
        G = 64
        GE_TEMP = 1.0
        ALPHA = 0.001
        SEQ_AUX = True
        NORM_TOPK = True
        COS_TEMP = 0.78
        CONS_ALPHA = 0.01
        LEAKY_SLOPE = 0.01
        EPS_COS = 1e-08

        def _leaky(x):
            return jnp.where(x >= 0, x, LEAKY_SLOPE * x)

        def _moe_forward(hidden_states, g, wt, wg, w_gate, w_up, w_down, sw_gate, sw_up, sw_down):
            b, s, h = hidden_states.shape
            x = hidden_states.reshape(-1, h)
            T = x.shape[0]
            logits_h = x @ wt.T
            logits_g = g @ wg.T
            logits_g = jnp.repeat(logits_g, s, axis=0)
            logits = (logits_h + logits_g / GE_TEMP) / (1.0 + 1.0 / GE_TEMP)
            scores = jax.nn.softmax(logits, axis=-1)
            topk_w, topk_idx = jax.lax.top_k(scores, K)
            if K > 1 and NORM_TOPK:
                topk_w = topk_w / (topk_w.sum(-1, keepdims=True) + 1e-20)
            onehot = jax.nn.one_hot(topk_idx.reshape(b, s * K), E, dtype=jnp.float32)
            ce = onehot.sum(1) / (s * K / E)
            aux_loss = (ce * scores.reshape(b, s, E).mean(1)).sum(1).mean() * ALPHA
            gp = _leaky(jnp.einsum('th,ehm->etm', x, w_gate))
            up = jnp.einsum('th,ehm->etm', x, w_up)
            y_all = jnp.einsum('etm,emh->eth', gp * up, w_down)
            y_sel = y_all[topk_idx, jnp.arange(T)[:, None], :]
            y = (y_sel * topk_w[..., None]).sum(1).reshape(b, s, h)
            p = _leaky(hidden_states @ sw_gate) * (hidden_states @ sw_up) @ sw_down
            y = y + p
            num = jnp.sum(y * p, -1)
            den = jnp.maximum(jnp.linalg.norm(y, axis=-1), EPS_COS) * jnp.maximum(jnp.linalg.norm(p, axis=-1), EPS_COS)
            closs = CONS_ALPHA * jnp.mean(num / den / (1.0 + COS_TEMP))
            return (y, aux_loss + closs)
        key = jax.random.key(seed)
        ks = jax.random.split(key, 12)
        sh = 1.0 / np.sqrt(H)
        sm = 1.0 / np.sqrt(M)
        ssm = 1.0 / np.sqrt(SM)
        sg = 1.0 / np.sqrt(G)
        return {'hidden_states': jax.random.normal(ks[0], (B, S, H), jnp.float32), 'g': jax.random.normal(ks[1], (B, G), jnp.float32), 'wt': jax.random.uniform(ks[2], (E, H), jnp.float32, -sh, sh), 'wg': jax.random.uniform(ks[3], (E, G), jnp.float32, -sg, sg), 'w_gate': jax.random.uniform(ks[4], (E, H, M), jnp.float32, -sh, sh), 'w_up': jax.random.uniform(ks[5], (E, H, M), jnp.float32, -sh, sh), 'w_down': jax.random.uniform(ks[6], (E, M, H), jnp.float32, -sm, sm), 'sw_gate': jax.random.uniform(ks[7], (H, SM), jnp.float32, -sh, sh), 'sw_up': jax.random.uniform(ks[8], (H, SM), jnp.float32, -sh, sh), 'sw_down': jax.random.uniform(ks[9], (SM, H), jnp.float32, -ssm, ssm)}
    _L1_cond_all = _L1_cond_setup()
    _L1_cond_in = {k: v for k, v in _L1_cond_all.items() if k in ('wt', 'wg', 'w_gate', 'w_up', 'w_down', 'sw_gate', 'sw_up', 'sw_down')}
    del _L1_cond_all
    return {'x': x, 'cond_64': cond_64, 'mask_BxS_bf1': mask_BxS_bf1, 'L0_cond_g_norm': _L0_cond_in['g_norm'], 'L0_cond_Wq': _L0_cond_in['Wq'], 'L0_cond_Wkv': _L0_cond_in['Wkv'], 'L0_cond_q_scale': _L0_cond_in['q_scale'], 'L0_cond_k_scale': _L0_cond_in['k_scale'], 'L0_cond_null_attn_bias': _L0_cond_in['null_attn_bias'], 'L0_cond_w0': _L0_cond_in['w0'], 'L0_cond_b0': _L0_cond_in['b0'], 'L0_cond_g0': _L0_cond_in['g0'], 'L0_cond_w1': _L0_cond_in['w1'], 'L0_cond_b1': _L0_cond_in['b1'], 'L0_cond_g1': _L0_cond_in['g1'], 'L0_cond_w2': _L0_cond_in['w2'], 'L0_cond_b2': _L0_cond_in['b2'], 'L0_cond_Wout': _L0_cond_in['Wout'], 'L0_cond_g_out': _L0_cond_in['g_out'], 'L1_cond_wt': _L1_cond_in['wt'], 'L1_cond_wg': _L1_cond_in['wg'], 'L1_cond_w_gate': _L1_cond_in['w_gate'], 'L1_cond_w_up': _L1_cond_in['w_up'], 'L1_cond_w_down': _L1_cond_in['w_down'], 'L1_cond_sw_gate': _L1_cond_in['sw_gate'], 'L1_cond_sw_up': _L1_cond_in['sw_up'], 'L1_cond_sw_down': _L1_cond_in['sw_down']}

def reference(x, cond_64, mask_BxS_bf1, L0_cond_g_norm, L0_cond_Wq, L0_cond_Wkv, L0_cond_q_scale, L0_cond_k_scale, L0_cond_null_attn_bias, L0_cond_w0, L0_cond_b0, L0_cond_g0, L0_cond_w1, L0_cond_b1, L0_cond_g1, L0_cond_w2, L0_cond_b2, L0_cond_Wout, L0_cond_g_out, L1_cond_wt, L1_cond_wg, L1_cond_w_gate, L1_cond_w_up, L1_cond_w_down, L1_cond_sw_gate, L1_cond_sw_up, L1_cond_sw_down):
    import jax
    import jax.numpy as jnp

    def _L0_cond_ref(x, mask, g_norm, Wq, Wkv, q_scale, k_scale, null_kv, null_attn_bias, w0, b0, g0, w1, b1, g1, w2, b2, Wout, g_out):
        import jax, jax.numpy as jnp
        import numpy as np
        DIM = 256
        HEADS = 16
        DIM_HEAD = 64
        SCALE = 8.0

        def ln(x, g, eps=1e-05):
            mean = x.mean(axis=-1, keepdims=True)
            var = ((x - mean) ** 2).mean(axis=-1, keepdims=True)
            return (x - mean) * jax.lax.rsqrt(var + eps) * g

        def l2norm(t):
            n = jnp.maximum(jnp.linalg.norm(t, axis=-1, keepdims=True), 1e-12)
            return t / n

        def rel_pos_bias(n, w0, b0, g0, w1, b1, g1, w2, b2, dtype):
            pos = jnp.arange(-n + 1, n, dtype=dtype)[:, None]
            h = jax.nn.silu(ln(pos @ w0 + b0, g0))
            h = jax.nn.silu(ln(h @ w1 + b1, g1))
            h = h @ w2 + b2
            i = jnp.arange(n)
            idx = i[:, None] - i[None, :] + n - 1
            bias = h[idx]
            return jnp.transpose(bias, (2, 0, 1))
        b, n, _ = x.shape
        xn = ln(x, g_norm)
        q = (xn @ Wq).reshape(b, n, HEADS, DIM_HEAD).transpose(0, 2, 1, 3)
        kv = xn @ Wkv
        k, v = (kv[..., :DIM_HEAD], kv[..., DIM_HEAD:])
        nk = jnp.broadcast_to(null_kv[0], (b, 1, DIM_HEAD))
        nv = jnp.broadcast_to(null_kv[1], (b, 1, DIM_HEAD))
        k = jnp.concatenate([nk, k], axis=1)
        v = jnp.concatenate([nv, v], axis=1)
        q = l2norm(q) * q_scale
        k = l2norm(k) * k_scale
        sim = jnp.einsum('bhid,bjd->bhij', q, k) * SCALE
        bias = rel_pos_bias(n, w0, b0, g0, w1, b1, g1, w2, b2, q.dtype)
        null_bias = jnp.broadcast_to(null_attn_bias[:, None, None], (HEADS, n, 1))
        attn_bias = jnp.concatenate([null_bias, bias], axis=-1)
        sim = sim + attn_bias
        neg = -jnp.finfo(sim.dtype).max
        causal = jnp.triu(jnp.ones((n, n + 1), dtype=bool), k=2)
        sim = jnp.where(causal, neg, sim)
        m = jnp.pad(mask, ((0, 0), (1, 0)), constant_values=True)[:, None, None, :]
        sim = jnp.where(m, sim, neg)
        attn = jax.nn.softmax(sim, axis=-1)
        out = jnp.einsum('bhij,bjd->bhid', attn, v)
        out = out.transpose(0, 2, 1, 3).reshape(b, n, HEADS * DIM_HEAD)
        return ln(out @ Wout, g_out)

    def _L1_cond_ref(hidden_states, g, wt, wg, w_gate, w_up, w_down, sw_gate, sw_up, sw_down):
        import jax, jax.numpy as jnp
        import numpy as np
        B, S, H = (4, 512, 256)
        E = 8
        M = 128
        K = 2
        N_SHARED = 2
        SM = M * N_SHARED
        G = 64
        GE_TEMP = 1.0
        ALPHA = 0.001
        SEQ_AUX = True
        NORM_TOPK = True
        COS_TEMP = 0.78
        CONS_ALPHA = 0.01
        LEAKY_SLOPE = 0.01
        EPS_COS = 1e-08

        def _leaky(x):
            return jnp.where(x >= 0, x, LEAKY_SLOPE * x)

        def _moe_forward(hidden_states, g, wt, wg, w_gate, w_up, w_down, sw_gate, sw_up, sw_down):
            b, s, h = hidden_states.shape
            x = hidden_states.reshape(-1, h)
            T = x.shape[0]
            logits_h = x @ wt.T
            logits_g = g @ wg.T
            logits_g = jnp.repeat(logits_g, s, axis=0)
            logits = (logits_h + logits_g / GE_TEMP) / (1.0 + 1.0 / GE_TEMP)
            scores = jax.nn.softmax(logits, axis=-1)
            topk_w, topk_idx = jax.lax.top_k(scores, K)
            if K > 1 and NORM_TOPK:
                topk_w = topk_w / (topk_w.sum(-1, keepdims=True) + 1e-20)
            onehot = jax.nn.one_hot(topk_idx.reshape(b, s * K), E, dtype=jnp.float32)
            ce = onehot.sum(1) / (s * K / E)
            aux_loss = (ce * scores.reshape(b, s, E).mean(1)).sum(1).mean() * ALPHA
            gp = _leaky(jnp.einsum('th,ehm->etm', x, w_gate))
            up = jnp.einsum('th,ehm->etm', x, w_up)
            y_all = jnp.einsum('etm,emh->eth', gp * up, w_down)
            y_sel = y_all[topk_idx, jnp.arange(T)[:, None], :]
            y = (y_sel * topk_w[..., None]).sum(1).reshape(b, s, h)
            p = _leaky(hidden_states @ sw_gate) * (hidden_states @ sw_up) @ sw_down
            y = y + p
            num = jnp.sum(y * p, -1)
            den = jnp.maximum(jnp.linalg.norm(y, axis=-1), EPS_COS) * jnp.maximum(jnp.linalg.norm(p, axis=-1), EPS_COS)
            closs = CONS_ALPHA * jnp.mean(num / den / (1.0 + COS_TEMP))
            return (y, aux_loss + closs)
        y, _ = _moe_forward(hidden_states, g, wt, wg, w_gate, w_up, w_down, sw_gate, sw_up, sw_down)
        return y
    x = x + _L0_cond_ref(x, mask_BxS_bf1, L0_cond_g_norm, L0_cond_Wq, L0_cond_Wkv, L0_cond_q_scale, L0_cond_k_scale, cond_64, L0_cond_null_attn_bias, L0_cond_w0, L0_cond_b0, L0_cond_g0, L0_cond_w1, L0_cond_b1, L0_cond_g1, L0_cond_w2, L0_cond_b2, L0_cond_Wout, L0_cond_g_out)
    x = x + _L1_cond_ref(x, cond_64, L1_cond_wt, L1_cond_wg, L1_cond_w_gate, L1_cond_w_up, L1_cond_w_down, L1_cond_sw_gate, L1_cond_sw_up, L1_cond_sw_down)
    return x

_drawn_inputs = setup_inputs


def setup_inputs(seed=0):
    import zlib

    import numpy as np

    out = dict(_drawn_inputs(seed))
    spreads = {'L0_cond_g_norm': (1.0, 0.2),
     'L0_cond_q_scale': (1.0, 0.2),
     'L0_cond_k_scale': (1.0, 0.2),
     'L0_cond_b0': (0.0, 0.268),
     'L0_cond_g0': (1.0, 0.6),
     'L0_cond_b1': (0.0, 0.332),
     'L0_cond_g1': (1.0, 0.6),
     'L0_cond_b2': (0.0, 0.429),
     'L0_cond_g_out': (1.0, 0.2)}
    factors = {}
    for name, (base, spread) in spreads.items():
        noise = np.random.default_rng([zlib.crc32(name.encode()), seed]).standard_normal(out[name].shape)
        drawn = base * np.exp(spread * noise) if base else spread * noise
        out[name] = jnp.asarray(drawn.astype(out[name].dtype))
    for name, factor in factors.items():
        out[name] = (out[name] * factor).astype(out[name].dtype)
    return out
```

```python
from contextlib import ExitStack

import numpy as np

import concourse.bass as bass
from concourse import mybir

ALU = mybir.AluOpType
ACT = mybir.ActivationFunctionType
AX = mybir.AxisListType.X
F32 = mybir.dt.float32
BF16 = mybir.dt.bfloat16
U8 = mybir.dt.uint8
U32 = mybir.dt.uint32
I32 = mybir.dt.int32

P = 128
B, N, D = 16, 256, 256
HEADS, DH = 16, 64
PAIRS = HEADS // 2
KC = D // P
E, SHARED = 8, 2
BLOCKS = E + SHARED
COND = 64
NULL_ROWS = 64
TOK = 512
TILES = TOK // P
BB = TOK // N
ROUNDS = B * N // TOK
GROUPS = 4
STEPS = 4
ALL = GROUPS * STEPS
GH = 2 * STEPS
KVN = 2 * DH + HEADS
LN_EPS = 1e-5
BIG = 1e30
LEAKY = 0.01
ORDER = list(range(E, BLOCKS)) + list(range(E))
WB_RING = 4
LAG = 4
AT_STEP = {0: 6, 2: 7, 16: 8, 18: 9}


class Events:

    def __init__(self, sem, per, base=0):
        self.sem, self.per, self.base = sem, per, base

    def at(self, r, c):
        return r * self.per + (c + self.base)


def need(eng, ev, r, c):
    value = ev.at(r, c)
    if isinstance(value, int) and value <= ev.base:
        return
    eng.wait_ge(ev.sem, value)


def stand(eng, waited):
    eng.sem_inc(waited, 1)


class Chain:

    def __init__(self, ev):
        self.ev, self.r, self.c = ev, 0, 0

    def start(self, r):
        self.r, self.c = r, 0

    def link(self, eng, ins):
        self.c += 1
        assert self.c <= self.ev.per
        ins.then_inc(self.ev.sem, 1)
        eng.wait_ge(self.ev.sem, self.ev.at(self.r, self.c))

    def end(self):
        assert self.c == self.ev.per, (self.c, self.ev.per)


def attention_moe(nc, x, condT, condR, mask, wq, wkv, wout, wgate, wup, wdown, wt, wgT, gnorm,
                  rows, smalls, w1, w2, out):
    wscr = nc.dram_tensor("wscr", (E, TOK), F32, kind="Internal")
    bscr = nc.dram_tensor("bscr", (HEADS, 2 * N), F32, kind="Internal")
    bscr2 = nc.dram_tensor("bscr2", (P, HEADS, N), F32, kind="Internal")
    x_t = x.rearrange("(r t p) d -> r p t d", t=TILES, p=P)
    out_t = out.rearrange("(r t p) d -> r p t d", t=TILES, p=P)

    with ExitStack() as ctx:
        def sb(name, shape, dt=F32):
            return ctx.enter_context(nc.sbuf_tensor(name, shape, dt))

        def ps(name, shape):
            return ctx.enter_context(nc.psum_tensor(name, shape, F32))

        def events(name, per, base=0):
            return Events(ctx.enter_context(nc.semaphore(name)), per, base)

        Wq = sb("Wq", [P, KC, HEADS * DH])
        Wkvn = sb("Wkvn", [P, KC, KVN])
        Wout = sb("Wout", [P, PAIRS, D])
        Wg = sb("Wg", [P, KC, BLOCKS, P])
        Wu = sb("Wu", [P, KC, BLOCKS, P])
        Wd = sb("Wd", [P, BLOCKS, D])
        Wt = sb("Wt", [P, KC, E])
        bias = sb("bias", [P, HEADS, N])
        null_bias = sb("null_bias", [P, HEADS])
        Unull = sb("Unull", [P, D])
        cond_logits = sb("cond_logits", [P, B, E])
        gout = sb("gout", [P, D])
        qk_scale = sb("qk_scale", [P, DH])
        ident = sb("ident", [P, P])
        ones_bf = sb("ones_bf", [P, P], BF16)
        neghalf = sb("neghalf", [P, HEADS])
        iota8 = sb("iota8", [P, E])
        xin = sb("xin", [P, TILES, D])
        xres = sb("xres", [P, TILES, D])
        xnT = sb("xnT", [P, KC, TOK])
        kvs = sb("kvs", [P, TILES, KVN])
        kd = sb("kd", [P, TILES, 2, DH])
        KB = sb("KB", [P, BB, 2, N])
        MK = sb("MK", [P, TOK], BF16)
        mask8 = sb("mask8", [1, TOK], U8)
        qs = sb("qs", [P, TILES, HEADS * DH])
        xn = qs[:, 0, :].rearrange("p (t d) -> p t d", t=TILES)
        yo = qs[:, 1, :].rearrange("p (t d) -> p t d", t=TILES)
        sq = sb("sq", [P, HEADS * DH])
        qT = sb("qT", [P, PAIRS, TOK])
        null_s = sb("null_s", [P, TILES, HEADS])
        T1 = [sb(f"T1_{i}", [P, GH, N + 1]) for i in range(2)]
        T0 = [sb(f"T0_{i}", [P, GH, P + 1]) for i in range(2)]
        low = [sb(f"low{i}", [P, 2, GH]) for i in range(2)]
        den = [sb(f"den{i}", [P, 2, GH]) for i in range(2)]
        rden = [sb(f"rden{i}", [P, 2, GH]) for i in range(2)]
        PT = [sb(f"PTs{i}", [P, 2, 3 * P]) for i in range(2)]
        PNT = sb("PNT", [P, TOK])
        stats = sb("stats", [P, TILES, 6])
        mv = sb("mv", [P, TILES, 2])
        ve = sb("ve", [P, TILES])
        rstd = sb("rstd", [P, TILES])
        stats2 = sb("stats2", [P, TILES, 6])
        mv2 = sb("mv2", [P, TILES, 2])
        ve2 = sb("ve2", [P, TILES])
        rstd2 = sb("rstd2", [P, TILES])
        ksq = sb("ksq", [P, TILES, DH])
        kss = sb("kss", [P, TILES])
        rk = sb("rk", [P, TILES])
        kn = sb("kn", [P, TILES, DH])
        qss = sb("qss", [P, TILES, HEADS])
        rq = sb("rq", [P, TILES, HEADS])
        yn = sq[:].rearrange("p (t d) -> p t d", t=TILES)
        x1 = sb("x1", [P, TILES, D])
        x1T = sb("x1T", [P, KC, TOK])
        leaky = [sb(f"leaky{i}", [P, TOK]) for i in range(2)]
        H = sb("H", [P, BLOCKS, TOK])
        Wb = sb("Wb", [P, WB_RING, TOK])
        WT = sb("WT", [E, TOK])
        lg = sb("lg", [P, TILES, E])
        lgx = sb("lgx", [P, TILES])
        lgc = sb("lgc", [P, TILES, E])
        lex = sb("lex", [P, TILES, E])
        lsum = sb("lsum", [P, TILES])
        lrec = sb("lrec", [P, TILES])
        score = sb("score", [P, TILES, E])
        top = sb("top", [P, TILES, E])
        topi = sb("topi", [P, TILES, E], U32)
        topf = sb("topf", [P, TILES, 2])
        oh1 = sb("oh1", [P, TILES, E])
        oh2 = sb("oh2", [P, TILES, E])
        tsum = sb("tsum", [P, TILES])
        trec = sb("trec", [P, TILES])
        wsel = sb("wsel", [P, TILES, E])
        flatH = H[:, :, :].rearrange("p b t -> p (b t)")
        rows_b = flatH[:, 0:5 * D].rearrange("p (n d) -> p n d", n=5)
        smalls_b = flatH[:, 1280:1536]
        w1s = flatH[:, 1536:2048].rearrange("p (c d) -> p c d", c=KC)
        w2s = flatH[:, 2048:2080].rearrange("p (c h) -> p c h", c=KC)
        ph = flatH[:, 2080:2592].rearrange("p (t d) -> p t d", t=2)
        pe = flatH[:, 2592:3104].rearrange("p (t d) -> p t d", t=2)
        phT = flatH[:, 3104:3616].rearrange("p (c n) -> p c n", c=KC)
        vn_flat = flatH[:, 3616:3616 + PAIRS * NULL_ROWS]
        vn_cols = vn_flat.rearrange("p (q m) -> p q m", q=PAIRS)
        relbuf = flatH[0:HEADS, 4128:4128 + 2 * N]
        misc = flatH[:, 4640:5120]
        vnull = misc[:, 0:1]
        gn = misc[:, 1:3]
        pos = misc[:, 3:5]
        pst = misc[:, 8:20].rearrange("p (t s) -> p t s", t=2)
        pmv = misc[:, 20:24].rearrange("p (t s) -> p t s", t=2)
        pve = misc[:, 24:26]
        prs = misc[:, 26:28]
        nss = misc[:, 28:29]
        nrs = misc[:, 29:30]
        knull = misc[:, 32:96]
        relb = misc[:, 96:128].rearrange("p (t h) -> p t h", t=2)
        wnull = misc[:, 128:160]
        ones64 = misc[0:COND, 160:288]
        condx = misc[0:COND, 288:416].rearrange("p (b e) -> p b e", b=B)
        condTs = misc[0:COND, 416:432]
        wgTs = misc[0:COND, 432:440]
        knsq = misc[:, 440:441]
        posi = sb("posi", [P, 2], I32)
        iota8i = sb("iota8i", [P, E], I32)
        ksq0 = kn[:, 0, :]
        wprod = qs[:, 0:2, :].rearrange("p c (h d) -> p (c h) d", h=HEADS)

        psS = ps("psS", [P, 2, 512])
        psT = ps("psT", [P, 2, 512])
        psO = ps("psO", [P, 512])
        psG = ps("psG", [P, 512])
        psU = ps("psU", [P, 512])
        psY = ps("psY", [P, 512])
        banks4 = [psS[:, 0, :], psS[:, 1, :], psT[:, 0, :], psT[:, 1, :]]

        ld_w = events("ld_w", 0)
        ld_small = events("ld_small", 0)
        pre_v = events("pre_v", 0)
        pre_p = events("pre_p", 0)
        pre_t = events("pre_t", 0)
        pre_a = events("pre_a", 0)
        pre_d = events("pre_d", 0)
        xin_in = events("xin_in", 16)
        xres_in = events("xres_in", 16)
        mask_in = events("mask_in", 16)
        wscr_in = events("wscr_in", 16, 16)
        wb_in = [events(f"wb_in{i}", 16 * (E // WB_RING)) for i in range(WB_RING)]
        out_in = events("out_in", 16, 16)
        ln_var = events("ln_var", 1)
        xn_done = events("xn_done", TILES)
        xnT_v = events("xnT_v", 1)
        mk_done = events("mk_done", 1)
        kss_done = events("kss_done", 1)
        kd_done = events("kd_done", 1)
        kb_v = events("kb_v", 1)
        qss_done = events("qss_done", TILES)
        qn_done = events("qn_done", TILES)
        qT_v = events("qT_v", TILES)
        s1_read = events("s1_read", GROUPS * STEPS)
        s0_read = events("s0_read", GROUPS * STEPS)
        rden_done = events("rden_done", ALL)
        pt0_done = events("pt0_done", GROUPS * STEPS)
        pn_done = events("pn_done", GROUPS)
        o_done = events("o_done", GROUPS * STEPS)
        y_var = events("y_var", 1)
        x1_done = events("x1_done", TILES)
        x1T_v = events("x1T_v", 1)
        lg_done = events("lg_done", 1)
        leaky_done = events("leaky_done", BLOCKS, 1)
        h_done = events("h_done", BLOCKS, 1)
        ysum = events("ysum", TILES, 1)
        vchain = {n: Chain(events("v_" + n, k)) for n, k in
                  (("ln1", 2), ("knorm", 3), ("null", 2), ("ln2", 2), ("x1", TILES), ("router", 14))}
        xnT_a = events("xnT_a", 1)
        kvs_done = events("kvs_done", 2)
        kb_a = events("kb_a", 1)
        sq_done = events("sq_done", TILES)
        qs_done = events("qs_done", TILES)
        qT_a = events("qT_a", TILES)
        exp_done = events("exp_done", GROUPS * STEPS)
        pt1_done = events("pt1_done", GROUPS * STEPS)
        x1T_a = events("x1T_a", 1)
        lex_done = events("lex_done", 1)
        wT_done = events("wT_done", 1)
        relu_done = events("relu_done", BLOCKS)
        rstd_done = events("rstd_done", 1)
        rk_done = events("rk_done", 1)
        rq_done = events("rq_done", TILES)
        norm_done = events("norm_done", ALL)
        rstd2_done = events("rstd2_done", 1)
        hw_done = events("hw_done", E, 1)
        xnT_ps = events("xnT_ps", 2)
        kv_ps = events("kv_ps", 2)
        kdT_ps = events("kdT_ps", 1)
        q_ps = events("q_ps", TILES)
        qT_ps = events("qT_ps", 2 * TILES)
        s1_ps = events("s1_ps", GROUPS * STEPS)
        s0_ps = events("s0_ps", GROUPS * STEPS)
        pt1_ps = events("pt1_ps", GROUPS * STEPS)
        pt0_ps = events("pt0_ps", GROUPS * STEPS)
        pv_ps = events("pv_ps", GROUPS * STEPS)
        wo_ps = events("wo_ps", TILES)
        x1T_ps = events("x1T_ps", 2)
        lg_ps = events("lg_ps", 1)
        wT_ps = events("wT_ps", 1)
        g_ps = events("g_ps", BLOCKS)
        u_ps = events("u_ps", BLOCKS)
        down_ps = events("down_ps", TILES)

        waited = ctx.enter_context(nc.semaphore("waited"))
        waited_sp = ctx.enter_context(nc.semaphore("waited_sp"))
        PRE_SMALL = 16 * 12
        V_CX, V_NSS, V_VAR0, V_SILU0, V_ACT0, V_HT0 = 17, 20, 28, 31, 34, 35
        V_VAR1, V_SILU1, V_ACT1, V_HT1, V_REL, V_RB, V_ALL = 41, 44, 47, 48, 50, 51, 60
        block = ctx.enter_context(nc.Block())

        @block.sync
        def _(sp):
            sp.sem_inc(wscr_in.sem, wscr_in.base)
            sp.sem_inc(out_in.sem, out_in.base)
            sp.dma_start(rows_b, rows[0:5, :].rearrange("n d -> (n d)").rearrange("(a m) -> a m", a=1)
                         .to_broadcast([P, 5 * D])).then_inc(ld_small.sem, 16)
            sp.dma_start(gout[:], rows[5:6, :].to_broadcast([P, D])).then_inc(ld_small.sem, 16)
            sp.dma_start(smalls_b[:, 0:224], smalls.to_broadcast([P, 224])).then_inc(ld_small.sem, 16)
            sp.dma_start(w1s, w1).then_inc(ld_small.sem, 16)
            sp.dma_start(w2s, w2).then_inc(ld_small.sem, 16)
            sp.dma_start(vnull[0:DH, :], condR[1:2, :].rearrange("a d -> d a")).then_inc(ld_small.sem, 16)
            sp.dma_start(vnull[DH:P, :], condR[1:2, :].rearrange("a d -> d a")).then_inc(ld_small.sem, 16)
            sp.dma_start(gn, gnorm).then_inc(ld_small.sem, 16)
            sp.dma_start(condTs, condT).then_inc(ld_small.sem, 16)
            sp.dma_start(wgTs, wgT).then_inc(ld_small.sem, 16)
            sp.dma_start(Wt[:], wt).then_inc(ld_small.sem, 16)
            sp.dma_start(Wkvn[:, :, 0:2 * DH], wkv).then_inc(ld_small.sem, 16)

            def load_norm_x(r):
                need(sp, xn_done, r - 1, TILES)
                stand(sp, waited_sp)
                sp.dma_start(xin[:], x_t[r]).then_inc(xin_in.sem, 16)

            def load_round(r):
                need(sp, mk_done, r - 1, 1)
                stand(sp, waited_sp)
                sp.dma_start(mask8[:], mask[:, bass.ds(r * TOK, TOK)]).then_inc(mask_in.sem, 16)
                need(sp, x1_done, r - 1, TILES)
                stand(sp, waited_sp)
                sp.dma_start(xres[:], x_t[r]).then_inc(xres_in.sem, 16)

            def experts(m):
                need(sp, hw_done, m - 1, E)
                stand(sp, waited_sp)
                need(sp, wT_done, m, 1)
                stand(sp, waited_sp)
                sp.dma_start(wscr.ap(), WT[:]).then_inc(wscr_in.sem, 16)
                sp.wait_ge(wscr_in.sem, wscr_in.at(m, 16))
                for e in range(E):
                    if e >= WB_RING:
                        need(sp, hw_done, m, e - WB_RING + 1)
                        stand(sp, waited_sp)
                    sp.dma_start(Wb[:, e % WB_RING, :], wscr.ap()[e:e + 1, :].to_broadcast([P, TOK])) \
                        .then_inc(wb_in[e % WB_RING].sem, 16)

            def store(m):
                need(sp, ysum, m, TILES)
                stand(sp, waited_sp)
                sp.dma_start(out_t[m], yo).then_inc(out_in.sem, 16)

            load_norm_x(0)
            load_round(0)
            for dst, src in ((Wq, wq), (Wg, wgate), (Wu, wup), (Wd, wdown), (Wout, wout)):
                sp.dma_start(dst[:], src).then_inc(ld_w.sem, 16)
            sp.wait_ge(pre_v.sem, V_RB)
            sp.dma_start(bscr.ap(), relbuf).then_inc(pre_d.sem, 16)
            sp.wait_ge(pre_d.sem, 16)
            sp.dma_start(bscr2.ap().rearrange("p h j -> h p j"),
                         bass.AP(tensor=bscr, offset=P - 1, ap=[[2 * N, HEADS], [-1, P], [1, N]])) \
                .then_inc(pre_d.sem, 16)
            sp.wait_ge(pre_d.sem, 32)
            sp.dma_start(bias[:], bscr2.ap()).then_inc(pre_d.sem, 16)
            load_norm_x(1)
            with sp.Fori(1, ROUNDS - 1) as r:
                load_round(r)
                experts(r - 1)
                load_norm_x(r + 1)
                store(r - 1)
            load_round(ROUNDS - 1)
            experts(ROUNDS - 2)
            store(ROUNDS - 2)
            experts(ROUNDS - 1)
            store(ROUNDS - 1)
            sp.wait_ge(out_in.sem, out_in.at(ROUNDS, 0))

        @block.gpsimd
        def _(pool):
            pool.sem_inc(hw_done.sem, hw_done.base)
            pool.memset(ident[:], 0.0).then_inc(pre_p.sem, 1)
            pool.memset(neghalf[:], -0.5).then_inc(pre_p.sem, 1)
            pool.iota(posi[:], pattern=[[-P, 2]], base=N - 1, channel_multiplier=-1).then_inc(pre_p.sem, 1)
            pool.iota(iota8i[:], pattern=[[1, E]], base=0, channel_multiplier=0).then_inc(pre_p.sem, 1)
            pool.wait_ge(pre_p.sem, 4)
            pool.affine_select(out=ident[:], in_=ident[:], compare_op=ALU.not_equal, fill=1.0, base=0,
                               pattern=[[-1, P]], channel_multiplier=1).then_inc(pre_p.sem, 1)
            pool.wait_ge(pre_p.sem, 5)
            pool.wait_ge(pre_v.sem, V_NSS)
            pool.tensor_tensor(nrs, nss, neghalf[:, 0:1], ALU.pow).then_inc(pre_p.sem, 1)
            for k in (V_VAR0, V_VAR1):
                pool.wait_ge(pre_v.sem, k)
                pool.tensor_tensor(prs, pve, neghalf[:, 0:2], ALU.pow).then_inc(pre_p.sem, 1)

            def norm_x(r):
                need(pool, ln_var, r, 1)
                pool.tensor_tensor(rstd[:], ve[:], neghalf[:, 0:TILES], ALU.pow).then_inc(rstd_done.sem, 1)

            def attention(r, moe, following):
                need(pool, kss_done, r, 1)
                pool.tensor_tensor(rk[:], kss[:], neghalf[:, 0:TILES], ALU.pow).then_inc(rk_done.sem, 1)
                for t in range(TILES):
                    need(pool, qss_done, r, t + 1)
                    pool.tensor_tensor(rq[:, t, :], qss[:, t, :], neghalf[:], ALU.pow).then_inc(rq_done.sem, 1)
                weighed = SHARED
                for n in range(ALL):
                    g, st = n // STEPS, n % STEPS
                    sl, hs = g % 2, slice(2 * st, 2 * st + 2)
                    need(pool, rden_done, r, n + 1)
                    pool.tensor_tensor(T1[sl][:, hs, :], T1[sl][:, hs, :], rden[sl][:, 1, hs].unsqueeze(2)
                                       .to_broadcast([P, 2, N + 1]), ALU.mult)
                    pool.tensor_tensor(T0[sl][:, hs, :], T0[sl][:, hs, :], rden[sl][:, 0, hs].unsqueeze(2)
                                       .to_broadcast([P, 2, P + 1]), ALU.mult).then_inc(norm_done.sem, 1)
                    if moe is not None and n % 2 == 1 and weighed < 8:
                        weigh(moe, weighed)
                        weighed += 1
                if moe is not None:
                    weigh(moe, 8)
                    weigh(moe, 9)
                need(pool, y_var, r, 1)
                pool.tensor_tensor(rstd2[:], ve2[:], neghalf[:, 0:TILES], ALU.pow).then_inc(rstd2_done.sem, 1)
                if following is not None:
                    norm_x(following)

            def weigh(m, k):
                e = ORDER[k]
                need(pool, h_done, m, k + 1)
                need(pool, wb_in[e % WB_RING], m, 16 * (e // WB_RING + 1))
                pool.tensor_tensor(H[:, e, :], H[:, e, :], Wb[:, e % WB_RING, :], ALU.mult) \
                    .then_inc(hw_done.sem, 1)

            norm_x(0)
            attention(0, None, 1)
            with pool.Fori(1, ROUNDS - 1) as r:
                attention(r, r - 1, r + 1)
            attention(ROUNDS - 1, ROUNDS - 2, None)
            for k in range(SHARED, BLOCKS):
                weigh(ROUNDS - 1, k)

        @block.scalar
        def _(act):
            for k, v in enumerate((V_SILU0, V_SILU1)):
                act.wait_ge(pre_v.sem, v)
                act.activation(pe, ph, ACT.Exp, scale=-1.0).then_inc(pre_a.sem, 1)

            def attention(r, moe):
                need(act, xnT_ps, r, 1)
                act.activation(xnT[:, 0, :], psT[:, 0, :], ACT.Copy).then_inc(xnT_a.sem, 1)
                if moe is not None:
                    route(moe)
                for n in range(2):
                    need(act, kv_ps, r, n + 1)
                    act.activation(kvs[:, 2 * n:2 * n + 2, :],
                                   psT[:, n, 0:2 * KVN].rearrange("p (t c) -> p t c", t=2), ACT.Copy) \
                        .then_inc(kvs_done.sem, 1)
                if moe is not None:
                    softmax(moe)
                for t in range(TILES):
                    if t == 1:
                        need(act, kdT_ps, r, 1)
                        act.activation(KB[0:DH, :, 0, :], psO[0:DH, :].rearrange("p (b j) -> p b j", b=BB),
                                       ACT.Copy).then_inc(kb_a.sem, 1)
                    if t == 3 and moe is not None:
                        weights(moe)
                    src = (psS if t % 2 == 0 else psT)[:, :, :].rearrange("p a c -> p (a c)")
                    need(act, q_ps, r, t + 1)
                    need(act, qss_done, r, t)
                    act.activation(sq[:], src, ACT.Square).then_inc(sq_done.sem, 1)
                    if t == 1 and moe is not None:
                        need(act, out_in, moe, 0)
                    act.activation(qs[:, t, :], src, ACT.Copy).then_inc(qs_done.sem, 1)
                    if moe is not None:
                        gate(moe, t)
                if moe is not None:
                    gate(moe, 4)
                for t in range(TILES):
                    need(act, qT_ps, r, 2 * t + 1)
                    act.activation(qT[:, 0:4, t * P:(t + 1) * P],
                                   banks4[2 * t % 4].rearrange("p (q i) -> p q i", q=4), ACT.Copy) \
                        .then_inc(qT_a.sem, 1)
                if moe is not None:
                    gate(moe, 5)
                for n in range(ALL + LAG):
                    if n < ALL:
                        exps(r, n // STEPS, n % STEPS)
                    if moe is not None and n in AT_STEP:
                        gate(moe, AT_STEP[n])
                    if n >= LAG:
                        turned(r, n - LAG)

            def exps(r, g, s):
                sl = g % 2
                n = g * STEPS + s
                need(act, s1_read, r, n + 1)
                for h in (2 * s, 2 * s + 1):
                    act.activation(T1[sl][:, h, :], T1[sl][:, h, :], ACT.Exp, scale=-1.0,
                                   bias=low[sl][:, 1, h:h + 1], accum_out=den[sl][:, 1, h:h + 1])
                need(act, s0_read, r, n + 1)
                for h in (2 * s, 2 * s + 1):
                    last = act.activation(T0[sl][:, h, :], T0[sl][:, h, :], ACT.Exp, scale=-1.0,
                                          bias=low[sl][:, 0, h:h + 1], accum_out=den[sl][:, 0, h:h + 1])
                last.then_inc(exp_done.sem, 1)

            def turned(r, n):
                need(act, pt1_ps, r, n + 1)
                need(act, pv_ps, r, n - 1)
                act.activation(PT[n % 2][:, :, P:3 * P], psT[:, 0, :].rearrange("p (h c) -> p h c", h=2),
                               ACT.Copy).then_inc(pt1_done.sem, 1)

            def route(m):
                need(act, x1T_ps, m, 1)
                act.activation(x1T[:, 0, :], psG[:], ACT.Copy).then_inc(x1T_a.sem, 1)

            def softmax(m):
                need(act, lg_done, m, 1)
                act.activation(lex[:], lgc[:], ACT.Exp, scale=0.5).then_inc(lex_done.sem, 1)

            def weights(m):
                need(act, wT_ps, m, 1)
                need(act, wscr_in, m - 1, 16)
                act.activation(WT[:], psY[0:E, :], ACT.Copy).then_inc(wT_done.sem, 1)

            def gate(m, k):
                need(act, g_ps, m, k + 1)
                need(act, h_done, m, max(k - 1, 0))
                act.activation(leaky[k % 2][:], psG[:], ACT.Relu, scale=(1 - LEAKY) / LEAKY) \
                    .then_inc(relu_done.sem, 1)

            attention(0, None)
            with act.Fori(1, ROUNDS) as r:
                attention(r, r - 1)
            route(ROUNDS - 1)
            softmax(ROUNDS - 1)
            weights(ROUNDS - 1)
            for k in range(BLOCKS):
                gate(ROUNDS - 1, k)

        @block.vector
        def _(dve):
            for ev in (leaky_done, h_done, ysum):
                dve.sem_inc(ev.sem, ev.base)
            count = [0]

            def pre(ins):
                count[0] += 1
                ins.then_inc(pre_v.sem, 1)
                dve.wait_ge(pre_v.sem, count[0])
                return count[0]

            for ap, v in ((KB[:], 0.0), (MK[:], 0.0), (ones_bf[:], 1.0), (PNT[:], 0.0), (Unull[:], 0.0),
                          (relbuf, BIG), (ones64, 1.0), (vn_cols, 0.0)):
                pre(dve.memset(ap, v))
            dve.wait_ge(pre_p.sem, 5)
            pre(dve.tensor_copy(pos, posi[:]))
            pre(dve.tensor_copy(iota8[:], iota8i[:]))
            dve.wait_ge(ld_small.sem, PRE_SMALL)
            b2_b, nb_b, qs_b, ks_b, kn_b = (smalls_b[:, a:b] for a, b in
                                            ((0, 16), (16, 32), (32, 96), (96, 160), (160, 224)))
            pre(dve.tensor_scalar(null_bias[:], nb_b, -1.0, None, ALU.mult))
            pre(dve.scalar_tensor_tensor(qk_scale[:], qs_b, -8.0, ks_b, ALU.mult, ALU.mult))
            for a in range(PAIRS // STEPS):
                for i in range(2):
                    first = (STEPS * NULL_ROWS + 32) * a + i
                    pre(dve.tensor_copy(
                        vn_flat[i * DH:(i + 1) * DH, first:first + (STEPS - 1) * (NULL_ROWS + 2) + 1:NULL_ROWS + 2],
                        vnull[i * DH:(i + 1) * DH, 0:1].to_broadcast([DH, STEPS])))
            n = pre(dve.tensor_tensor(condx, condTs.unsqueeze(2).to_broadcast([COND, B, E]),
                                      wgTs.unsqueeze(1).to_broadcast([COND, B, E]), ALU.mult))
            assert n == V_CX, n
            pre(dve.tensor_tensor(ksq0, kn_b, kn_b, ALU.mult))
            pre(dve.tensor_reduce(knsq, ksq0, AX, ALU.add))
            n = pre(dve.tensor_scalar(nss, knsq, 1e-24, None, ALU.max))
            assert n == V_NSS, n
            dve.wait_ge(pre_p.sem, 6)
            pre(dve.scalar_tensor_tensor(knull, kn_b, nrs, qk_scale[:], ALU.mult, ALU.mult))
            for t in range(2):
                pre(dve.scalar_tensor_tensor(ph[:, t, :], rows_b[:, 0, :], pos[:, t:t + 1], rows_b[:, 1, :],
                                             ALU.mult, ALU.add))
            for layer in range(2):
                for t in range(2):
                    pre(dve.bn_stats(pst[:, t, :], ph[:, t, :]))
                    pre(dve.bn_aggr(pmv[:, t, :], pst[:, t, :]))
                n = pre(dve.tensor_scalar(pve, pmv[:, :, 1], LN_EPS, None, ALU.add))
                assert n == (V_VAR0, V_VAR1)[layer], n
                dve.wait_ge(pre_p.sem, 7 + layer)
                for t in range(2):
                    pre(dve.tensor_scalar(ph[:, t, :], ph[:, t, :], pmv[:, t, 0:1], prs[:, t:t + 1],
                                          ALU.subtract, ALU.mult))
                n = pre(dve.tensor_tensor(ph, ph, rows_b[:, 2 + 2 * layer, :].unsqueeze(1)
                                          .to_broadcast([P, 2, D]), ALU.mult))
                assert n == (V_SILU0, V_SILU1)[layer], n
                dve.wait_ge(pre_a.sem, 1 + layer)
                pre(dve.tensor_scalar(pe, pe, 1.0, None, ALU.add))
                pre(dve.reciprocal(pe, pe))
                n = pre(dve.tensor_tensor(ph, ph, pe, ALU.mult))
                assert n == (V_ACT0, V_ACT1)[layer], n
                dve.wait_ge(pre_t.sem, 2 + 2 * layer)
                n = pre(dve.tensor_copy(phT.rearrange("p c n -> p (c n)"), psS[:, layer, :]))
                assert n == (V_HT0, V_HT1)[layer], n
                dve.wait_ge(pre_t.sem, 3 + 2 * layer)
                if layer == 0:
                    pre(dve.tensor_tensor(ph, psT[:, 0, :].rearrange("p (t d) -> p t d", t=2),
                                          rows_b[:, 3, :].unsqueeze(1).to_broadcast([P, 2, D]), ALU.add))
                else:
                    pre(dve.tensor_tensor(relb, psT[:, 1, 0:32].rearrange("p (t h) -> p t h", t=2),
                                          b2_b.unsqueeze(1).to_broadcast([P, 2, HEADS]), ALU.add))
                    n = pre(dve.tensor_scalar(relb, relb, -1.0, None, ALU.mult))
                    assert n == V_REL, n
            dve.wait_ge(pre_t.sem, 6)
            n = pre(dve.tensor_copy(relbuf[:, 0:N], psO[0:HEADS, 0:N]))
            assert n == V_RB, n
            dve.wait_ge(pre_t.sem, 1)
            pre(dve.tensor_copy(cond_logits[:].rearrange("p b e -> p (b e)"), psG[:, 0:B * E]))
            dve.wait_ge(ld_w.sem, 80)
            for c in range(KC):
                pre(dve.tensor_scalar(Wq[:, c, :], Wq[:, c, :], gn[:, c:c + 1], None, ALU.mult))
                pre(dve.tensor_scalar(Wkvn[:, c, 0:2 * DH], Wkvn[:, c, 0:2 * DH], gn[:, c:c + 1], None, ALU.mult))
            pre(dve.tensor_tensor(wprod, Wq[:].rearrange("p c (h d) -> p (c h) d", h=HEADS),
                                  knull.unsqueeze(1).to_broadcast([P, KC * HEADS, DH]), ALU.mult))
            pre(dve.tensor_reduce(wnull, wprod, AX, ALU.add))
            pre(dve.tensor_copy(Wkvn[:, :, 2 * DH:], wnull.rearrange("p (c h) -> p c h", c=KC)))
            dve.wait_ge(pre_t.sem, 7)
            n = pre(dve.tensor_copy(Unull[0:NULL_ROWS, :], psU[0:NULL_ROWS, 0:D]))
            assert n == V_ALL, n
            dve.wait_ge(pre_d.sem, 48)

            def norm_stats(r):
                ch = vchain["ln1"]
                ch.start(r)
                need(dve, xin_in, r, 16)
                for t in range(TILES):
                    ins = dve.bn_stats(stats[:, t, :], xin[:, t, :])
                ch.link(dve, ins)
                stand(dve, waited)
                for t in range(TILES):
                    ins = dve.bn_aggr(mv[:, t, :], stats[:, t, :])
                ch.link(dve, ins)
                ch.end()
                dve.tensor_scalar(ve[:], mv[:, :, 1], LN_EPS, None, ALU.add).then_inc(ln_var.sem, 1)

            def norm_x(r):
                need(dve, rstd_done, r, 1)
                for t in range(TILES):
                    dve.tensor_scalar(xn[:, t, :], xin[:, t, :], mv[:, t, 0:1], rstd[:, t:t + 1],
                                      ALU.subtract, ALU.mult).then_inc(xn_done.sem, 1)

            def attention(r, moe, following):
                need(dve, xnT_ps, r, 2)
                dve.tensor_copy(xnT[:, 1, :], psT[:, 1, :]).then_inc(xnT_v.sem, 1)
                need(dve, mask_in, r, 16)
                dve.tensor_scalar(MK[0:1, :], mask8[:], -BIG, BIG, ALU.mult, ALU.add).then_inc(mk_done.sem, 1)
                if moe is not None:
                    need(dve, x1T_ps, moe, 2)
                    dve.tensor_copy(x1T[:, 1, :], psU[:]).then_inc(x1T_v.sem, 1)
                ch = vchain["knorm"]
                ch.start(r)
                need(dve, kvs_done, r, 2)
                ch.link(dve, dve.tensor_tensor(ksq[:], kvs[:, :, 0:DH], kvs[:, :, 0:DH], ALU.mult))
                ch.link(dve, dve.tensor_reduce(kss[:], ksq[:], AX, ALU.add))
                dve.tensor_scalar(kss[:], kss[:], 1e-24, None, ALU.max).then_inc(kss_done.sem, 1)
                need(dve, rk_done, r, 1)
                ch.link(dve, dve.tensor_tensor(kn[:], kvs[:, :, 0:DH], rk[:].unsqueeze(2)
                                               .to_broadcast([P, TILES, DH]), ALU.mult))
                ch.end()
                for i in range(2):
                    ins = dve.tensor_tensor(kd[:, :, i, :], kn[:], qk_scale[:].unsqueeze(1)
                                            .to_broadcast([P, TILES, DH]), ALU.mult)
                ins.then_inc(kd_done.sem, 1)
                if moe is not None:
                    router(moe)
                for t in range(TILES):
                    if t == 1:
                        need(dve, kdT_ps, r, 1)
                        dve.tensor_copy(KB[DH:P, :, 1, :], psO[DH:P, :].rearrange("p (b j) -> p b j", b=BB)) \
                            .then_inc(kb_v.sem, 1)
                    need(dve, sq_done, r, t + 1)
                    dve.tensor_reduce(qss[:, t, :], sq[:].rearrange("p (h d) -> p h d", h=HEADS), AX, ALU.add) \
                        .then_inc(qss_done.sem, 1)
                    if moe is not None:
                        hidden(moe, t)
                    if t >= 1:
                        scale_q(r, t - 1)
                scale_q(r, TILES - 1)
                ch = vchain["null"]
                ch.start(r)
                ch.link(dve, dve.tensor_tensor(null_s[:], kvs[:, :, 2 * DH:], rq[:], ALU.mult))
                ch.link(dve, dve.tensor_tensor(null_s[:], null_s[:], null_bias[:].unsqueeze(1)
                                               .to_broadcast([P, TILES, HEADS]), ALU.add))
                ch.end()
                if moe is not None:
                    hidden(moe, 4)
                for t in range(TILES):
                    need(dve, qT_ps, r, 2 * t + 2)
                    dve.tensor_copy(qT[:, 4:8, t * P:(t + 1) * P],
                                    banks4[(2 * t + 1) % 4].rearrange("p (q i) -> p q i", q=4)) \
                        .then_inc(qT_v.sem, 1)
                if moe is not None:
                    hidden(moe, 5)
                for n in range(ALL + LAG + 1):
                    if n < ALL:
                        if n % STEPS == 0:
                            null_scores(r, n // STEPS)
                        scores(r, n // STEPS, n % STEPS)
                    if moe is not None and n in AT_STEP:
                        hidden(moe, AT_STEP[n])
                    if 1 <= n <= ALL:
                        rdens(r, n - 1)
                    if LAG <= n < ALL + LAG:
                        turned(r, n - LAG)
                        if (n - LAG) % STEPS == STEPS - 1:
                            null_turned(r, (n - LAG) // STEPS)
                    if n > LAG:
                        head_out(r, n - LAG - 1)
                ch = vchain["ln2"]
                ch.start(r)
                for t in range(TILES):
                    need(dve, wo_ps, r, t // 2 * 2 + 2)
                    ins = dve.bn_stats(stats2[:, t, :], psS[:, t // 2, (t % 2) * D:(t % 2 + 1) * D])
                ch.link(dve, ins)
                stand(dve, waited)
                for t in range(TILES):
                    ins = dve.bn_aggr(mv2[:, t, :], stats2[:, t, :])
                ch.link(dve, ins)
                ch.end()
                dve.tensor_scalar(ve2[:], mv2[:, :, 1], LN_EPS, None, ALU.add).then_inc(y_var.sem, 1)
                if following is not None:
                    norm_stats(following)
                ch = vchain["x1"]
                ch.start(r)
                need(dve, rstd2_done, r, 1)
                need(dve, xres_in, r, 16)
                for t in range(TILES):
                    ch.link(dve, dve.scalar_tensor_tensor(yn[:, t, :], psS[:, t // 2, (t % 2) * D:(t % 2 + 1) * D],
                                                          mv2[:, t, 0:1], gout[:], ALU.subtract, ALU.mult))
                if following is not None:
                    norm_x(following)
                for t in range(TILES):
                    if moe is not None:
                        sums(moe, t)
                        need(dve, ysum, moe, t + 1)
                    dve.scalar_tensor_tensor(x1[:, t, :], yn[:, t, :], rstd2[:, t:t + 1], xres[:, t, :],
                                             ALU.mult, ALU.add).then_inc(x1_done.sem, 1)
                ch.end()

            def rdens(r, n):
                need(dve, exp_done, r, n + 1)
                sl, hs = n // STEPS % 2, slice(2 * (n % STEPS), 2 * (n % STEPS) + 2)
                dve.reciprocal(rden[sl][:, :, hs], den[sl][:, :, hs]).then_inc(rden_done.sem, 1)

            def scale_q(r, t):
                need(dve, rq_done, r, t + 1)
                need(dve, qs_done, r, t + 1)
                q3 = qs[:, t, :].rearrange("p (h d) -> p h d", h=HEADS)
                dve.tensor_tensor(q3, q3, rq[:, t, :].unsqueeze(2).to_broadcast([P, HEADS, DH]), ALU.mult) \
                    .then_inc(qn_done.sem, 1)

            def null_scores(r, g):
                sl, bb, h0 = g % 2, g // 2, GH * (g % 2)
                need(dve, pt1_ps, r, STEPS * (g - 1))
                need(dve, pt0_ps, r, STEPS * (g - 1))
                for tile, T, n in ((1, T1, N), (0, T0, P)):
                    dve.tensor_copy(T[sl][:, :, n:n + 1],
                                    null_s[:, 2 * bb + tile, h0:h0 + GH].unsqueeze(2))

            def scores(r, g, s):
                sl, bb, h0 = g % 2, g // 2, GH * (g % 2)
                n = g * STEPS + s + 1
                need(dve, s1_ps, r, n)
                stand(dve, waited)
                for i in range(2):
                    h = 2 * s + i
                    ins = dve.tensor_tensor_reduce(
                        T1[sl][:, h, 0:N], psS[:, 0, i * N:(i + 1) * N], bias[:, h0 + h, :], 1.0,
                        null_s[:, 2 * bb + 1, h0 + h:h0 + h + 1], ALU.add, ALU.min, low[sl][:, 1, h:h + 1])
                ins.then_inc(s1_read.sem, 1)
                need(dve, s0_ps, r, n)
                stand(dve, waited)
                for i in range(2):
                    h = 2 * s + i
                    ins = dve.tensor_tensor_reduce(
                        T0[sl][:, h, 0:P], psS[:, 1, i * P:(i + 1) * P], bias[:, h0 + h, P:N], 1.0,
                        null_s[:, 2 * bb, h0 + h:h0 + h + 1], ALU.add, ALU.min, low[sl][:, 0, h:h + 1])
                ins.then_inc(s0_read.sem, 1)

            def turned(r, n):
                need(dve, pt0_ps, r, n + 1)
                need(dve, pv_ps, r, n - 1)
                dve.tensor_copy(PT[n % 2][:, :, 0:P], psT[:, 1, 0:2 * P].rearrange("p (h c) -> p h c", h=2)) \
                    .then_inc(pt0_done.sem, 1)

            def null_turned(r, g):
                p0 = 32 * (g % 2)
                dve.tensor_copy(PNT[p0:p0 + GH, (g // 2) * N:(g // 2 + 1) * N], psT[0:GH, 1, 2 * P:4 * P]) \
                    .then_inc(pn_done.sem, 1)

            def head_out(r, n):
                g, s = n // STEPS, n % STEPS
                need(dve, pv_ps, r, n + 1)
                dve.tensor_copy(qT[:, STEPS * (g % 2) + s, (g // 2) * N:(g // 2 + 1) * N], psO[:, 0:N]) \
                    .then_inc(o_done.sem, 1)

            def router(m):
                ch = vchain["router"]
                ch.start(m)
                need(dve, lg_ps, m, 1)
                ch.link(dve, dve.tensor_tensor(
                    lg[:].rearrange("p (b t) e -> p b t e", b=BB),
                    psY[:, 0:TILES * E].rearrange("p (b t e) -> p b t e", b=BB, e=E),
                    cond_logits[:, bass.ds(m * BB, BB), :].unsqueeze(2).to_broadcast([P, BB, TILES // BB, E]),
                    ALU.add))
                ch.link(dve, dve.tensor_reduce(lgx[:], lg[:], AX, ALU.max))
                dve.tensor_tensor(lgc[:], lg[:], lgx[:].unsqueeze(2).to_broadcast([P, TILES, E]),
                                  ALU.subtract).then_inc(lg_done.sem, 1)
                need(dve, lex_done, m, 1)
                ch.link(dve, dve.tensor_reduce(lsum[:], lex[:], AX, ALU.add))
                ch.link(dve, dve.reciprocal(lrec[:], lsum[:]))
                ch.link(dve, dve.tensor_tensor(score[:], lex[:], lrec[:].unsqueeze(2)
                                               .to_broadcast([P, TILES, E]), ALU.mult))
                stand(dve, waited)
                for t in range(TILES):
                    ins = dve.max(top[:, t, :], score[:, t, :])
                ch.link(dve, ins)
                stand(dve, waited)
                for t in range(TILES):
                    ins = dve.max_index(topi[:, t, :], top[:, t, :], score[:, t, :])
                ch.link(dve, ins)
                ch.link(dve, dve.tensor_copy(topf[:], topi[:, :, 0:2]))
                io = iota8[:].unsqueeze(1).to_broadcast([P, TILES, E])
                ch.link(dve, dve.tensor_tensor(oh1[:], io, topf[:, :, 0:1].to_broadcast([P, TILES, E]),
                                               ALU.is_equal))
                ch.link(dve, dve.tensor_tensor(oh2[:], io, topf[:, :, 1:2].to_broadcast([P, TILES, E]),
                                               ALU.is_equal))
                dve.tensor_tensor(tsum[:].unsqueeze(2), top[:, :, 0:1], top[:, :, 1:2], ALU.add)
                ch.link(dve, dve.tensor_tensor(oh1[:], oh1[:], oh2[:], ALU.add))
                ch.link(dve, dve.tensor_scalar(tsum[:], tsum[:], 1e-20, None, ALU.add))
                dve.reciprocal(trec[:], tsum[:])
                ch.link(dve, dve.tensor_tensor(wsel[:], oh1[:], score[:], ALU.mult))
                ch.link(dve, dve.tensor_tensor(oh2[:], wsel[:], trec[:].unsqueeze(2)
                                               .to_broadcast([P, TILES, E]), ALU.mult))
                ch.end()

            def hidden(m, k):
                need(dve, relu_done, m, k + 1)
                dve.tensor_tensor(leaky[k % 2][:], psG[:], leaky[k % 2][:], ALU.add).then_inc(leaky_done.sem, 1)
                need(dve, u_ps, m, k + 1)
                need(dve, leaky_done, m, k + 1)
                dve.scalar_tensor_tensor(H[:, ORDER[k], :], psU[:], LEAKY, leaky[k % 2][:],
                                         ALU.mult, ALU.mult).then_inc(h_done.sem, 1)

            def sums(m, t):
                need(dve, down_ps, m, t + 1)
                dve.tensor_tensor(yo[:, t, :], x1[:, t, :], (psY, psG, psU, psY)[t][:, 0:D], ALU.add) \
                    .then_inc(ysum.sem, 1)

            norm_stats(0)
            norm_x(0)
            attention(0, None, 1)
            with dve.Fori(1, ROUNDS - 1) as r:
                attention(r, r - 1, r + 1)
            attention(ROUNDS - 1, ROUNDS - 2, None)
            m = ROUNDS - 1
            need(dve, x1T_ps, m, 2)
            dve.tensor_copy(x1T[:, 1, :], psU[:]).then_inc(x1T_v.sem, 1)
            router(m)
            for k in range(BLOCKS):
                hidden(m, k)
            for t in range(TILES):
                sums(m, t)

        @block.tensor
        def _(te):
            te.wait_ge(pre_v.sem, V_CX)
            te.wait_ge(pre_p.sem, 5)
            te.matmul(psG[:, 0:B * E], ones64, condx.rearrange("p b e -> p (b e)"), start=True, stop=True) \
                .then_inc(pre_t.sem, 1)
            for layer in range(2):
                te.wait_ge(pre_v.sem, (V_ACT0, V_ACT1)[layer])
                for t in range(2):
                    for c in range(KC):
                        mm = te.transpose(psS[:, layer, c * N + t * P:c * N + (t + 1) * P],
                                          ph[:, t, c * P:(c + 1) * P], ident[:])
                mm.then_inc(pre_t.sem, 1)
                te.wait_ge(pre_v.sem, (V_HT0, V_HT1)[layer])
                w, n = ((w1s, D), (w2s, HEADS))[layer]
                for t in range(2):
                    for c in range(KC):
                        mm = te.matmul(psT[:, layer, t * n:(t + 1) * n], phT[:, c, t * P:(t + 1) * P],
                                       w[:, c, :], start=(c == 0), stop=(c == KC - 1))
                mm.then_inc(pre_t.sem, 1)
            te.wait_ge(pre_v.sem, V_REL)
            for t in range(2):
                mm = te.transpose(psO[0:HEADS, t * P:(t + 1) * P], relb[:, t, :], ident[:])
            mm.then_inc(pre_t.sem, 1)
            te.wait_ge(ld_w.sem, 80)
            for p in range(PAIRS):
                mm = te.matmul(psU[0:NULL_ROWS, 0:D], vn_cols[:, p, :], Wout[:, p, :], start=(p == 0),
                               stop=(p == PAIRS - 1))
            mm.then_inc(pre_t.sem, 1)
            te.wait_ge(pre_v.sem, V_ALL)

            def attention(r, moe):
                need(te, xn_done, r, TILES)
                for c in range(KC):
                    for t in range(TILES):
                        mm = te.transpose(psT[:, c, t * P:(t + 1) * P], xn[:, t, c * P:(c + 1) * P], ident[:])
                    mm.then_inc(xnT_ps.sem, 1)
                if moe is not None:
                    turn_x1(moe)
                need(te, xnT_a, r, 1)
                need(te, xnT_v, r, 1)
                for t in range(TILES):
                    for c in range(KC):
                        mm = te.matmul(psT[:, t // 2, (t % 2) * KVN:(t % 2 + 1) * KVN],
                                       xnT[:, c, t * P:(t + 1) * P], Wkvn[:, c, :],
                                       start=(c == 0), stop=(c == KC - 1))
                    if t % 2 == 1:
                        mm.then_inc(kv_ps.sem, 1)
                if moe is not None:
                    logits(moe)
                need(te, x1_done, r - 1, TILES)
                for t in range(TILES):
                    if t == 1:
                        need(te, kvs_done, r, 2)
                        need(te, kd_done, r, 1)
                        for tt in range(TILES):
                            mm = te.transpose(psO[:, tt * P:(tt + 1) * P],
                                              kd[:, tt, :, :].rearrange("p a d -> p (a d)"), ident[:])
                        mm.then_inc(kdT_ps.sem, 1)
                    if t == 3 and moe is not None:
                        turn_weights(moe)
                    if t >= 2:
                        need(te, qs_done, r, t - 1)
                    bank = psS if t % 2 == 0 else psT
                    for half in range(2):
                        for c in range(KC):
                            mm = te.matmul(bank[:, half, :], xnT[:, c, t * P:(t + 1) * P],
                                           Wq[:, c, half * 512:(half + 1) * 512],
                                           start=(c == 0), stop=(c == KC - 1))
                    mm.then_inc(q_ps.sem, 1)
                    if moe is not None:
                        expert(moe, t)
                if moe is not None:
                    expert(moe, 4)
                need(te, qs_done, r, TILES)
                for n in range(2 * TILES):
                    t, half = n // 2, n % 2
                    need(te, qn_done, r, t + 1)
                    if n >= 4:
                        need(te, qT_a if half == 0 else qT_v, r, t - 1)
                    for q in range(4):
                        mm = te.transpose(banks4[n % 4][:, q * P:(q + 1) * P],
                                          qs[:, t, (4 * half + q) * P:(4 * half + q + 1) * P], ident[:])
                    mm.then_inc(qT_ps.sem, 1)
                if moe is not None:
                    expert(moe, 5)
                need(te, qT_a, r, TILES)
                need(te, qT_v, r, TILES)
                need(te, kb_a, r, 1)
                need(te, kb_v, r, 1)
                need(te, mk_done, r, 1)
                for n in range(ALL + LAG + 1):
                    if n < ALL:
                        score(r, n // STEPS, n % STEPS)
                    if moe is not None and n in AT_STEP:
                        expert(moe, AT_STEP[n])
                    if LAG <= n < ALL + LAG:
                        turn(r, n - LAG)
                    if n > LAG:
                        value(r, n - LAG - 1)
                need(te, o_done, r, GROUPS * STEPS)
                need(te, pn_done, r, GROUPS)
                need(te, s1_read, r, GROUPS * STEPS)
                need(te, s0_read, r, GROUPS * STEPS)
                for t in range(TILES):
                    dst = psS[:, t // 2, (t % 2) * D:(t % 2 + 1) * D]
                    for p in range(PAIRS):
                        te.matmul(dst, qT[:, p, t * P:(t + 1) * P], Wout[:, p, :], start=(p == 0), stop=False)
                    te.matmul(dst, PNT[:, t * P:(t + 1) * P], Unull[:], start=False, stop=True) \
                        .then_inc(wo_ps.sem, 1)
                if moe is not None:
                    down(moe)

            def score(r, g, s):
                bb, p = g // 2, STEPS * (g % 2) + s
                n = g * STEPS + s
                q0 = bb * N
                need(te, s1_read, r, n)
                te.matmul(psS[:, 0, :], qT[:, p, q0 + P:q0 + N], KB[:, bb, :, :].rearrange("p h j -> p (h j)"),
                          start=True, stop=False)
                te.matmul(psS[:, 0, :], ones_bf[:], MK[:, q0:q0 + N].unsqueeze(1).to_broadcast([P, 2, N]),
                          start=False, stop=True).then_inc(s1_ps.sem, 1)
                need(te, s0_read, r, n)
                te.matmul(psS[:, 1, 0:2 * P], qT[:, p, q0:q0 + P], KB[:, bb, :, 0:P], start=True, stop=False)
                te.matmul(psS[:, 1, 0:2 * P], ones_bf[:], MK[:, q0:q0 + P].unsqueeze(1).to_broadcast([P, 2, P]),
                          start=False, stop=True).then_inc(s0_ps.sem, 1)

            def turn(r, n):
                g, s = n // STEPS, n % STEPS
                sl = g % 2
                need(te, norm_done, r, n + 1)
                need(te, pt1_done, r, n)
                for i in range(2):
                    for j in range(2):
                        mm = te.transpose(psT[:, 0, (2 * i + j) * P:(2 * i + j + 1) * P],
                                          T1[sl][:, 2 * s + i, j * P:(j + 1) * P], ident[:])
                mm.then_inc(pt1_ps.sem, 1)
                need(te, pt0_done, r, n)
                if s == 0:
                    need(te, pn_done, r, g)
                for i in range(2):
                    mm = te.transpose(psT[:, 1, i * P:(i + 1) * P], T0[sl][:, 2 * s + i, 0:P], ident[:])
                if s == STEPS - 1:
                    te.transpose(psT[0:GH, 1, 2 * P:3 * P], T0[sl][:, :, P], ident[:])
                    mm = te.transpose(psT[0:GH, 1, 3 * P:4 * P], T1[sl][:, :, N], ident[:])
                mm.then_inc(pt0_ps.sem, 1)

            def value(r, n):
                bb = n // STEPS // 2
                need(te, pt1_done, r, n + 1)
                need(te, pt0_done, r, n + 1)
                need(te, o_done, r, n)
                for i in range(2):
                    te.matmul(psO[i * DH:(i + 1) * DH, 0:N], kvs[:, 2 * bb, DH:2 * DH], PT[n % 2][:, i, 0:N],
                              start=True, stop=False)
                for i in range(2):
                    mm = te.matmul(psO[i * DH:(i + 1) * DH, P:N], kvs[:, 2 * bb + 1, DH:2 * DH],
                                   PT[n % 2][:, i, N:N + P], start=False, stop=True)
                mm.then_inc(pv_ps.sem, 1)

            def turn_x1(m):
                need(te, x1_done, m, TILES)
                need(te, ysum, m - 1, TILES)
                for c, bank in ((0, psG), (1, psU)):
                    for t in range(TILES):
                        mm = te.transpose(bank[:, t * P:(t + 1) * P], x1[:, t, c * P:(c + 1) * P], ident[:])
                    mm.then_inc(x1T_ps.sem, 1)

            def logits(m):
                need(te, x1T_a, m, 1)
                need(te, x1T_v, m, 1)
                for t in range(TILES):
                    for c in range(KC):
                        mm = te.matmul(psY[:, t * E:(t + 1) * E], x1T[:, c, t * P:(t + 1) * P], Wt[:, c, :],
                                       start=(c == 0), stop=(c == KC - 1))
                mm.then_inc(lg_ps.sem, 1)

            def turn_weights(m):
                te.wait_ge(vchain["router"].ev.sem, vchain["router"].ev.at(m, vchain["router"].ev.per))
                for t in range(TILES):
                    mm = te.transpose(psY[0:E, t * P:(t + 1) * P], oh2[:, t, :], ident[:])
                mm.then_inc(wT_ps.sem, 1)

            def expert(m, k):
                e = ORDER[k]
                need(te, leaky_done, m, k)
                for c in range(KC):
                    mm = te.matmul(psG[:], Wg[:, c, e, :], x1T[:, c, :], start=(c == 0), stop=(c == KC - 1))
                mm.then_inc(g_ps.sem, 1)
                need(te, h_done, m, k)
                for c in range(KC):
                    mm = te.matmul(psU[:], Wu[:, c, e, :], x1T[:, c, :], start=(c == 0), stop=(c == KC - 1))
                mm.then_inc(u_ps.sem, 1)

            def down(m):
                need(te, leaky_done, m, BLOCKS)
                need(te, h_done, m, BLOCKS)
                need(te, hw_done, m, E)
                need(te, wT_done, m, 1)
                for t in range(TILES):
                    if t == TILES - 1:
                        need(te, ysum, m, 1)
                    for k, e in enumerate(ORDER):
                        mm = te.matmul((psY, psG, psU, psY)[t][:, 0:D], H[:, e, t * P:(t + 1) * P], Wd[:, e, :],
                                       start=(k == 0), stop=(k == BLOCKS - 1))
                    mm.then_inc(down_ps.sem, 1)

            attention(0, None)
            with te.Fori(1, ROUNDS) as r:
                attention(r, r - 1)
            m = ROUNDS - 1
            turn_x1(m)
            logits(m)
            turn_weights(m)
            for k in range(BLOCKS):
                expert(m, k)
            down(m)


def kernel(**a):
    import concourse.bacc as bacc
    from concourse.bass_utils import run_bass_kernel_spmd

    a = {k: np.asarray(v) for k, v in a.items()}

    def chunks(w):
        return w.reshape(-1, P, w.shape[-1]).transpose(1, 0, 2)

    def blocks(w, shared):
        both = np.concatenate([w, shared.reshape(D, SHARED, P).transpose(1, 0, 2)])
        return both.reshape(BLOCKS, KC, P, P).transpose(2, 1, 0, 3)

    cond = a["cond_64"]
    arrays = {
        "x": a["x"].reshape(B * N, D),
        "condT": cond.T,
        "condR": cond,
        "mask": a["mask_BxS_bf1"].reshape(1, B * N).view(np.uint8),
        "wq": chunks(a["L0_cond_Wq"]),
        "wkv": chunks(a["L0_cond_Wkv"]),
        "wout": chunks(a["L0_cond_Wout"]),
        "wgate": blocks(a["L1_cond_w_gate"], a["L1_cond_sw_gate"]),
        "wup": blocks(a["L1_cond_w_up"], a["L1_cond_sw_up"]),
        "wdown": np.concatenate([a["L1_cond_w_down"], a["L1_cond_sw_down"].reshape(SHARED, P, D)]).transpose(1, 0, 2),
        "wt": chunks(a["L1_cond_wt"].T),
        "wgT": a["L1_cond_wg"].T,
        "gnorm": a["L0_cond_g_norm"].reshape(KC, P).T,
        "rows": np.stack([a["L0_cond_w0"][0], a["L0_cond_b0"], a["L0_cond_g0"], a["L0_cond_b1"],
                          a["L0_cond_g1"], a["L0_cond_g_out"]]),
        "smalls": np.concatenate([a["L0_cond_b2"], a["L0_cond_null_attn_bias"], a["L0_cond_q_scale"],
                                  a["L0_cond_k_scale"], cond[0]]).reshape(1, -1),
        "w1": chunks(a["L0_cond_w1"]),
        "w2": chunks(a["L0_cond_w2"]),
    }
    nc = bacc.Bacc("TRN2", target_bir_lowering=False, num_devices=1)
    feeds, args = {}, []
    for name, v in arrays.items():
        v = np.ascontiguousarray(v)
        feeds["in_" + name] = v
        args.append(nc.dram_tensor("in_" + name, v.shape, mybir.dt.from_np(v.dtype), kind="ExternalInput").ap())
    out = nc.dram_tensor("out", (B * N, D), F32, kind="ExternalOutput").ap()
    attention_moe(nc, *args, out)
    r = run_bass_kernel_spmd(nc, [feeds], core_ids=[0])
    return r.results[0]["out"].reshape(B, N, D)
```

```python
from contextlib import ExitStack

import numpy as np

import concourse.bass as bass
from concourse import mybir

ALU = mybir.AluOpType
ACT = mybir.ActivationFunctionType
AX = mybir.AxisListType.X
F32 = mybir.dt.float32
BF16 = mybir.dt.bfloat16
F32R = mybir.dt.float32r
U8 = mybir.dt.uint8
U32 = mybir.dt.uint32
I32 = mybir.dt.int32

P = 128
B, N, D = 16, 256, 256
HEADS, DH = 16, 64
PAIRS = HEADS // 2
KC = D // P
E, SHARED = 8, 2
BLOCKS = E + SHARED
COND = 64
NULL_ROWS = 64
TOK = 512
TILES = TOK // P
BB = TOK // N
ROUNDS = B * N // TOK
GROUPS = 4
STEPS = 4
ALL = GROUPS * STEPS
GH = 2 * STEPS
KVN = 2 * DH + HEADS
LN_EPS = 1e-5
BIG = 1e30
LEAKY = 0.01
ORDER = list(range(E, BLOCKS)) + list(range(E))
WB_RING = 2
FIRST_WEIGHTS = (1, 2, 0)
H_RING = 3
W_RING = 3
POOL_TILES = 1
TURN_LAG = 3
VALUE_LAG = 5
NORM_AT = 8
UNITS_AT = {0: (4, 5), 2: (6, 7)}
GATE_AT = {1: 3, 3: 4, 5: 5, 7: 6, 10: 7, 12: 8, 14: 9}
UP_AT = {n + 1: k for n, k in GATE_AT.items()}
DOWN_AT = {2: 1, 4: 2, 6: 3, 9: 4, 11: 5, 13: 6, 16: 7, 18: 8, 19: 9}


def products(te, dst, a, b, start, stop):
    (a_hi, a_lo), (b_hi, b_lo) = a, b
    te.matmul(dst, a_hi, b_hi, start=start, stop=False)
    te.matmul(dst, a_lo, b_hi, start=False, stop=False)
    return te.matmul(dst, a_hi, b_lo, start=False, stop=stop)


class Events:

    def __init__(self, sem, per, base=0):
        self.sem, self.per, self.base = sem, per, base

    def at(self, r, c):
        return r * self.per + (c + self.base)


def need(eng, ev, r, c):
    value = ev.at(r, c)
    if isinstance(value, int) and value <= ev.base:
        return
    eng.wait_ge(ev.sem, value)


def stand(eng, waited):
    eng.sem_inc(waited, 1)


class Chain:

    def __init__(self, ev):
        self.ev, self.r, self.c = ev, 0, 0

    def start(self, r):
        self.r, self.c = r, 0

    def link(self, eng, ins):
        self.c += 1
        assert self.c <= self.ev.per
        ins.then_inc(self.ev.sem, 1)
        eng.wait_ge(self.ev.sem, self.ev.at(self.r, self.c))

    def end(self):
        assert self.c == self.ev.per, (self.c, self.ev.per)


def attention_moe(nc, x, condT, condR, mask, wq, wkv, wout, wgu, wdown, wt, wgT, gnorm,
                  rows, smalls, w1, w2, out):
    wscr = nc.dram_tensor("wscr", (E, TOK), F32, kind="Internal")
    wexp = nc.dram_tensor("wexp", (BLOCKS, P, 2, 2, KC, P), F32, kind="Internal")
    bscr = nc.dram_tensor("bscr", (HEADS, 2 * N), F32, kind="Internal")
    bscr2 = nc.dram_tensor("bscr2", (P, HEADS, N), F32, kind="Internal")
    x_t = x.rearrange("(r t p) d -> r p t d", t=TILES, p=P)
    out_t = out.rearrange("(r t p) d -> r p t d", t=TILES, p=P)

    with ExitStack() as ctx:
        def sb(name, shape, dt=F32):
            return ctx.enter_context(nc.sbuf_tensor(name, shape, dt))

        def ps(name, shape):
            return ctx.enter_context(nc.psum_tensor(name, shape, F32))

        def events(name, per, base=0):
            return Events(ctx.enter_context(nc.semaphore(name)), per, base)

        PARTS = ("hi", "lo")
        Wall = [sb(f"Wall_{part}", [P, KC, E + KVN + HEADS * DH], F32R) for part in PARTS]
        KV0, Q0 = E, E + KVN
        Wout = [sb(f"Wout_{part}", [P, PAIRS, D], F32R) for part in PARTS]
        Wd = sb("Wd", [P, BLOCKS, D])
        Wt = sb("Wt", [P, KC, E])
        bias = sb("bias", [P, HEADS, N])
        null_bias = sb("null_bias", [P, HEADS])
        Unull = sb("Unull", [P, D])
        cond_logits = sb("cond_logits", [P, B, E])
        gout = sb("gout", [P, D])
        qk_scale = sb("qk_scale", [P, DH])
        ident = sb("ident", [P, P])
        ones_bf = sb("ones_bf", [P, P], BF16)
        neghalf = sb("neghalf", [P, HEADS])
        iota8 = sb("iota8", [P, E])
        xin = sb("xin", [P, TILES, D])
        xres = sb("xres", [P, TILES, D])
        xnT = [sb(f"xnT_{part}", [P, KC, TOK], F32R) for part in PARTS]
        kvs = sb("kvs", [P, TILES, KVN])
        kd = sb("kd", [P, TILES, 2, DH])
        KB = [sb(f"KB_{part}", [P, BB, 2, N], F32R) for part in PARTS]
        MK = sb("MK", [P, TOK], BF16)
        mask8 = sb("mask8", [1, TOK], U8)
        T_SIZE = 2 * GH * (N + 1 + P + 1)
        work = sb("work", [P, T_SIZE])
        T1_SIZE = GH * (N + 1)
        qs = [work[:, a:a + HEADS * DH] for a in (0, HEADS * DH, T1_SIZE, T1_SIZE + HEADS * DH)]
        yo = qs[1].rearrange("p (t d) -> p t d", t=TILES)
        sq = work[:, 2 * GH * (N + 1):2 * GH * (N + 1) + HEADS * DH]
        qT = [sb(f"qT_{part}", [P, PAIRS, TOK], F32R) for part in PARTS]
        null_s = sb("null_s", [P, TILES, HEADS])
        T1 = [work[:, i * GH * (N + 1):(i + 1) * GH * (N + 1)].rearrange("p (h j) -> p h j", h=GH)
              for i in range(2)]
        T0 = [work[:, 2 * GH * (N + 1) + i * GH * (P + 1):2 * GH * (N + 1) + (i + 1) * GH * (P + 1)]
              .rearrange("p (h j) -> p h j", h=GH) for i in range(2)]
        low = [sb(f"low{i}", [P, 2, GH]) for i in range(2)]
        den = [sb(f"den{i}", [P, 2, GH]) for i in range(2)]
        rden = [sb(f"rden{i}", [P, 2, GH]) for i in range(2)]
        PT = [sb(f"PTs{i}", [P, 2, 3 * P]) for i in range(2)]
        PNT = sb("PNT", [P, TOK])
        stats = sb("stats", [P, TILES, 6])
        mv = sb("mv", [P, TILES, 2])
        ve = sb("ve", [P, TILES])
        rstd = sb("rstd", [P, TILES])
        stats2 = sb("stats2", [P, TILES, 6])
        mv2 = sb("mv2", [P, TILES, 2])
        ve2 = sb("ve2", [P, TILES])
        rstd2 = sb("rstd2", [P, TILES])
        ksq = sb("ksq", [P, TILES, DH])
        kss = sb("kss", [P, TILES])
        rk = sb("rk", [P, TILES])
        kn = sb("kn", [P, TILES, DH])
        qss = sb("qss", [P, TILES, HEADS])
        rq = sb("rq", [P, TILES, HEADS])
        x1 = sb("x1", [P, TILES, D])
        x1T = [sb(f"x1T_{part}", [P, KC, TOK], F32R) for part in PARTS]
        Wgu = sb("Wgu", [P, W_RING, 2, 2, KC, P], F32R)
        leaky = [sb(f"leaky{i}", [P, TOK]) for i in range(2)]
        H = sb("H", [P, H_RING, TOK])
        Wb = sb("Wb", [P, WB_RING, TOK])
        WT = sb("WT", [E, TOK])
        lg = sb("lg", [P, TILES, E])
        lgx = sb("lgx", [P, TILES])
        lgc = sb("lgc", [P, TILES, E])
        lex = sb("lex", [P, TILES, E])
        lsum = sb("lsum", [P, TILES])
        lrec = sb("lrec", [P, TILES])
        score = sb("score", [P, TILES, E])
        top = sb("top", [P, TILES, E])
        topi = sb("topi", [P, TILES, E], U32)
        topf = sb("topf", [P, TILES, 2])
        oh1 = sb("oh1", [P, TILES, E])
        oh2 = sb("oh2", [P, TILES, E])
        tsum = sb("tsum", [P, TILES])
        trec = sb("trec", [P, TILES])
        wsel = sb("wsel", [P, TILES, E])
        flatb = bias[:, :, :].rearrange("p h j -> p (h j)")
        flatH = H[:, :, :].rearrange("p b t -> p (b t)")
        rows_b = flatb[:, 0:5 * D].rearrange("p (n d) -> p n d", n=5)
        w1s = flatb[:, 1280:1792].rearrange("p (c d) -> p c d", c=KC)
        ph = flatb[:, 1792:2304].rearrange("p (t d) -> p t d", t=2)
        pe = flatb[:, 2304:2816].rearrange("p (t d) -> p t d", t=2)
        phT = flatb[:, 2816:3328].rearrange("p (c n) -> p c n", c=KC)
        smalls_b = flatb[:, 3328:3584]
        w2s = flatb[:, 3584:3616].rearrange("p (c h) -> p c h", c=KC)
        misc = flatH[:, 0:512]
        vn_flat = flatH[:, 512:512 + PAIRS * NULL_ROWS]
        vn_cols = vn_flat.rearrange("p (q m) -> p q m", q=PAIRS)
        relbuf = flatH[0:HEADS, 1024:1024 + 2 * N]
        vnull = misc[:, 0:1]
        gn = misc[:, 1:3]
        pos = misc[:, 3:5]
        pst = misc[:, 8:20].rearrange("p (t s) -> p t s", t=2)
        pmv = misc[:, 20:24].rearrange("p (t s) -> p t s", t=2)
        pve = misc[:, 24:26]
        prs = misc[:, 26:28]
        nss = misc[:, 28:29]
        nrs = misc[:, 29:30]
        knull = misc[:, 32:96]
        relb = misc[:, 96:128].rearrange("p (t h) -> p t h", t=2)
        wnull = misc[:, 128:160]
        ones64 = misc[0:COND, 160:288]
        condx = misc[0:COND, 288:416].rearrange("p (b e) -> p b e", b=B)
        condTs = misc[0:COND, 416:432]
        wgTs = misc[0:COND, 432:440]
        knsq = misc[:, 440:441]
        posi = sb("posi", [P, 2], I32)
        iota8i = sb("iota8i", [P, E], I32)
        ksq0 = kn[:, 0, :]
        Wq_in = work[:, 0:KC * HEADS * DH].rearrange("p (c k) -> p c k", c=KC)
        Wout_in = work[:, 2048:4096].rearrange("p (q d) -> p q d", q=PAIRS)
        wprod = x1[:, :, :].rearrange("p t d -> p (t d)").rearrange("p (h d) -> p h d", h=HEADS)
        Wkvn_in = work[:, 4096:4096 + KC * KVN].rearrange("p (c k) -> p c k", c=KC)

        psS = ps("psS", [P, 2, 512])
        psT = ps("psT", [P, 2, 512])
        psO = ps("psO", [P, 512])
        psG = ps("psG", [P, 512])
        psY = ps("psY", [P, 2, 512])
        wo_banks = [psS[:, 0, 0:D], psS[:, 1, 0:D], psG[:, 0:D], psO[:, 0:D]]
        banks4 = [psT[:, 0, :], psT[:, 1, :], psS[:, 0, :], psS[:, 1, :]]

        def gate_bank(k, alone):
            return psT[:, k % 2, :] if alone else psG[:]

        def up_bank(k, alone):
            return psS[:, k % 2, :] if alone else psG[:]

        def q_bank(n):
            return banks4[n if n < 4 else n % 2]

        ld_rows = events("ld_rows", 0)
        ld_q = events("ld_q", 0)
        ld_out = events("ld_out", 0)
        ld_down = events("ld_down", 0)
        ld_small = events("ld_small", 0)
        pre_v = events("pre_v", 0)
        pre_p = events("pre_p", 0)
        pre_t = events("pre_t", 0)
        pre_a = events("pre_a", 0)
        w_scaled = events("w_scaled", 0)
        w_lead = events("w_lead", 0)
        w_trail = events("w_trail", 0)
        kb_zero = events("kb_zero", 0)
        pre_d = events("pre_d", 0)
        wraw_in = [events(f"wraw_in{i}", 0) for i in range(H_RING)]
        lead_done = events("lead_done", 0)
        parts_done = events("parts_done", 0)
        parts_out = [events(f"parts_out{i}", 0) for i in range(W_RING)]
        xin_in = events("xin_in", 16)
        xres_in = events("xres_in", 16)
        mask_in = events("mask_in", 16)
        wscr_in = events("wscr_in", 16, 16)
        wb_in = [events(f"wb_in{i}", 16 * (E // WB_RING)) for i in range(WB_RING)]
        out_in = events("out_in", 16, 16)
        wgu_ld = [events(f"wgu_ld{i}", 16 * len(range(i, BLOCKS, W_RING))) for i in range(W_RING)]
        ln_var = events("ln_var", 1)
        xn_done = events("xn_done", TILES)
        xnT_v = events("xnT_v", 3)
        mk_done = events("mk_done", 1)
        kss_done = events("kss_done", 1)
        kd_done = events("kd_done", 1)
        kb_v = events("kb_v", 3)
        qss_done = events("qss_done", TILES)
        qn_done = events("qn_done", TILES - POOL_TILES)
        qT_v = events("qT_v", 2 * TILES)
        s1_read = events("s1_read", GROUPS * STEPS)
        s0_read = events("s0_read", GROUPS * STEPS)
        rden_done = events("rden_done", ALL)
        pt0_done = events("pt0_done", GROUPS * STEPS)
        pn_done = events("pn_done", GROUPS)
        o_done = events("o_done", GROUPS * STEPS)
        y_var = events("y_var", TILES)
        x1_done = events("x1_done", TILES)
        x1T_v = events("x1T_v", 3)
        lg_done = events("lg_done", 1)
        leaky_done = events("leaky_done", BLOCKS, 1)
        h_done = events("h_done", BLOCKS, 1)
        ysum = events("ysum", TILES, 1)
        vchain = {n: Chain(events("v_" + n, k)) for n, k in
                  (("ln1", 2), ("knorm", 3), ("null", 4), ("ln2", 2 * TILES), ("x1", TILES), ("router", 14))}
        xnT_a = events("xnT_a", 1)
        kvs_done = events("kvs_done", 2)
        kb_a = events("kb_a", 1)
        sq_done = events("sq_done", TILES)
        qs_done = events("qs_done", TILES)
        qT_a = events("qT_a", 2 * TILES)
        exp_done = events("exp_done", GROUPS * STEPS)
        pt1_done = events("pt1_done", GROUPS * STEPS)
        x1T_a = events("x1T_a", 1)
        lex_done = events("lex_done", 1)
        wT_done = events("wT_done", 1)
        o_lead = events("o_lead", ALL)
        gate_out = events("gate_out", BLOCKS)
        rstd_done = events("rstd_done", 1)
        rk_done = events("rk_done", 1)
        rq_done = events("rq_done", TILES)
        qn_pool = events("qn_pool", POOL_TILES)
        norm_done = events("norm_done", ALL)
        rstd2_done = events("rstd2_done", TILES)
        hw_done = events("hw_done", E, 1)
        xnT_ps = events("xnT_ps", 2)
        kv_ps = events("kv_ps", 2)
        kdT_ps = events("kdT_ps", 1)
        q_ps = events("q_ps", TILES)
        qT_ps = events("qT_ps", 2 * TILES)
        s1_ps = events("s1_ps", GROUPS * STEPS)
        s0_ps = events("s0_ps", GROUPS * STEPS)
        pt1_ps = events("pt1_ps", GROUPS * STEPS)
        pt0_ps = events("pt0_ps", GROUPS * STEPS)
        pv_ps = events("pv_ps", GROUPS * STEPS)
        wo_ps = events("wo_ps", TILES)
        x1T_ps = events("x1T_ps", 2)
        lg_ps = events("lg_ps", 1)
        wT_ps = events("wT_ps", 1)
        g_ps = events("g_ps", BLOCKS)
        u_ps = events("u_ps", BLOCKS, W_RING)
        h_used = events("h_used", BLOCKS - 1)
        down_ps = events("down_ps", TILES)

        waited = ctx.enter_context(nc.semaphore("waited"))
        waited_sp = ctx.enter_context(nc.semaphore("waited_sp"))
        PRE_SMALL = 16 * 11
        V_VAR0, V_CX, V_NSS, V_SILU0, V_ACT0, V_HT0 = 17, 24, 27, 30, 34, 35
        V_VAR1, V_SILU1, V_ACT1, V_HT1, V_REL, V_RB, V_ALL = 46, 49, 52, 57, 61, 62, 62
        block = ctx.enter_context(nc.Block())

        def scale_q(eng, r, t, done):
            need(eng, rq_done, r, t + 1)
            need(eng, qs_done, r, t + 1)
            q3 = qs[t].rearrange("p (h d) -> p h d", h=HEADS)
            eng.tensor_tensor(q3, q3, rq[:, t, :].unsqueeze(2).to_broadcast([P, HEADS, DH]), ALU.mult) \
                .then_inc(done.sem, 1)

        @block.sync
        def _(sp):
            sp.sem_inc(wscr_in.sem, wscr_in.base)
            sp.sem_inc(out_in.sem, out_in.base)
            sp.dma_start(rows_b, rows[0:5, :].rearrange("n d -> (n d)").rearrange("(a m) -> a m", a=1)
                         .to_broadcast([P, 5 * D])).then_inc(ld_rows.sem, 16)
            sp.dma_start(gout[:], rows[5:6, :].to_broadcast([P, D])).then_inc(ld_small.sem, 16)
            sp.dma_start(smalls_b[:, 0:224], smalls.to_broadcast([P, 224])).then_inc(ld_small.sem, 16)
            sp.dma_start(w1s, w1).then_inc(ld_small.sem, 16)
            sp.dma_start(w2s, w2).then_inc(ld_small.sem, 16)
            sp.dma_start(vnull[0:DH, :], condR[1:2, :].rearrange("a d -> d a")).then_inc(ld_small.sem, 16)
            sp.dma_start(vnull[DH:P, :], condR[1:2, :].rearrange("a d -> d a")).then_inc(ld_small.sem, 16)
            sp.dma_start(gn, gnorm).then_inc(ld_small.sem, 16)
            sp.dma_start(condTs, condT).then_inc(ld_small.sem, 16)
            sp.dma_start(wgTs, wgT).then_inc(ld_small.sem, 16)
            sp.dma_start(Wt[:], wt).then_inc(ld_small.sem, 16)
            sp.dma_start(Wkvn_in[:, :, 0:2 * DH], wkv).then_inc(ld_small.sem, 16)

            def load_norm_x(r):
                need(sp, xnT_ps, r - 1, 2)
                stand(sp, waited_sp)
                sp.dma_start(xin[:], x_t[r]).then_inc(xin_in.sem, 16)

            def load_round(r):
                need(sp, mk_done, r - 1, 1)
                stand(sp, waited_sp)
                sp.dma_start(mask8[:], mask[:, bass.ds(r * TOK, TOK)]).then_inc(mask_in.sem, 16)
                need(sp, x1_done, r - 1, TILES)
                stand(sp, waited_sp)
                sp.dma_start(xres[:], x_t[r]).then_inc(xres_in.sem, 16)

            def load_weights(m, k):
                former = k - W_RING if k >= W_RING else max(range(k, BLOCKS, W_RING)) - BLOCKS
                need(sp, u_ps, m, former + 1)
                stand(sp, waited_sp)
                sp.dma_start(Wgu[:, k % W_RING].bitcast(F32), wexp.ap()[ORDER[k]]).then_inc(wgu_ld[k % W_RING].sem, 16)

            def experts(m):
                for k in range(W_RING, 2 * W_RING):
                    load_weights(m, k)
                need(sp, hw_done, m - 1, E)
                stand(sp, waited_sp)
                need(sp, wT_done, m, 1)
                stand(sp, waited_sp)
                sp.dma_start(wscr.ap(), WT[:]).then_inc(wscr_in.sem, 16)
                sp.wait_ge(wscr_in.sem, wscr_in.at(m, 16))
                for e in range(E):
                    if e >= WB_RING:
                        need(sp, hw_done, m, e - WB_RING + 1)
                        stand(sp, waited_sp)
                    sp.dma_start(Wb[:, e % WB_RING, :], wscr.ap()[e:e + 1, :].to_broadcast([P, TOK])) \
                        .then_inc(wb_in[e % WB_RING].sem, 16)
                    if 1 <= e <= BLOCKS - 2 * W_RING:
                        load_weights(m, 2 * W_RING + e - 1)

            def store(m):
                need(sp, ysum, m, TILES)
                stand(sp, waited_sp)
                sp.dma_start(out_t[m], yo).then_inc(out_in.sem, 16)

            sp.dma_start(Wq_in, wq).then_inc(ld_q.sem, 16)
            load_norm_x(0)
            load_round(0)
            sp.dma_start(Wout_in, wout).then_inc(ld_out.sem, 16)
            sp.dma_start(Wd[:], wdown).then_inc(ld_down.sem, 16)
            sp.wait_ge(pre_v.sem, V_RB)
            sp.dma_start(bscr.ap(), relbuf).then_inc(pre_d.sem, 16)
            sp.wait_ge(pre_d.sem, 16)
            sp.dma_start(bscr2.ap().rearrange("p h j -> h p j"),
                         bass.AP(tensor=bscr, offset=P - 1, ap=[[2 * N, HEADS], [-1, P], [1, N]])) \
                .then_inc(pre_d.sem, 16)
            sp.wait_ge(pre_d.sem, 32)
            sp.dma_start(bias[:], bscr2.ap()).then_inc(pre_d.sem, 16)
            load_norm_x(1)
            sp.wait_ge(pre_v.sem, V_ALL)
            for e in range(BLOCKS + 2):
                if e < BLOCKS:
                    if e >= H_RING:
                        sp.wait_ge(parts_done.sem, e - H_RING + 1)
                    sp.dma_start(H[:, e % H_RING, :], wgu[e].rearrange("p w c m -> p (w c m)")) \
                        .then_inc(wraw_in[e % H_RING].sem, 16)
                if e >= 2:
                    sp.wait_ge(parts_done.sem, e - 1)
                    sp.dma_start(wexp.ap()[e - 2], Wgu[:, (e - 2) % W_RING].bitcast(F32)) \
                        .then_inc(parts_out[(e - 2) % W_RING].sem, 16)
            for i in range(W_RING):
                sp.wait_ge(parts_out[i].sem, 16 * len(range(i, BLOCKS, W_RING)))
            for k in FIRST_WEIGHTS:
                load_weights(0, k)
            with sp.Fori(1, ROUNDS - 1) as r:
                load_norm_x(r + 1)
                load_round(r)
                experts(r - 1)
                for k in FIRST_WEIGHTS:
                    load_weights(r, k)
                store(r - 1)
            load_round(ROUNDS - 1)
            experts(ROUNDS - 2)
            for k in FIRST_WEIGHTS:
                load_weights(ROUNDS - 1, k)
            store(ROUNDS - 2)
            experts(ROUNDS - 1)
            store(ROUNDS - 1)
            sp.wait_ge(out_in.sem, out_in.at(ROUNDS, 0))

        @block.gpsimd
        def _(pool):
            pool.sem_inc(hw_done.sem, hw_done.base)
            pool.memset(ident[:], 0.0).then_inc(pre_p.sem, 1)
            pool.memset(neghalf[:], -0.5).then_inc(pre_p.sem, 1)
            pool.iota(posi[:], pattern=[[-P, 2]], base=N - 1, channel_multiplier=-1).then_inc(pre_p.sem, 1)
            pool.iota(iota8i[:], pattern=[[1, E]], base=0, channel_multiplier=0).then_inc(pre_p.sem, 1)
            pool.wait_ge(pre_p.sem, 4)
            pool.affine_select(out=ident[:], in_=ident[:], compare_op=ALU.not_equal, fill=1.0, base=0,
                               pattern=[[-1, P]], channel_multiplier=1).then_inc(pre_p.sem, 1)
            pool.wait_ge(pre_p.sem, 5)
            for k, out_, in_ in ((V_VAR0, prs, pve), (V_NSS, nrs, nss), (V_VAR1, prs, pve)):
                if k == V_VAR1:
                    for n, (src, hi, lo) in enumerate(((Wout_in, Wout[0][:], Wout[1][:]),
                                                       (Wq_in, *(part[:, :, Q0:] for part in Wall)))):
                        pool.wait_ge(w_lead.sem, n + 1)
                        pool.tensor_tensor(lo, src, hi.bitcast(F32), ALU.subtract).then_inc(w_trail.sem, 1)
                pool.wait_ge(pre_v.sem, k)
                pool.tensor_tensor(out_, in_, neghalf[:, 0:out_.shape[-1]], ALU.pow).then_inc(pre_p.sem, 1)

            def norm_x(r):
                need(pool, ln_var, r, 1)
                pool.tensor_tensor(rstd[:], ve[:], neghalf[:, 0:TILES], ALU.pow).then_inc(rstd_done.sem, 1)

            def attention(r, moe, following):
                need(pool, kss_done, r, 1)
                pool.tensor_tensor(rk[:], kss[:], neghalf[:, 0:TILES], ALU.pow).then_inc(rk_done.sem, 1)
                for t in range(TILES):
                    need(pool, qss_done, r, t + 1)
                    pool.tensor_tensor(rq[:, t, :], qss[:, t, :], neghalf[:], ALU.pow).then_inc(rq_done.sem, 1)
                    if t < POOL_TILES:
                        scale_q(pool, r, t, qn_pool)
                for n in range(ALL):
                    g, st = n // STEPS, n % STEPS
                    sl, hs = g % 2, slice(2 * st, 2 * st + 2)
                    if moe is not None and n in UP_AT:
                        if UP_AT[n] == SHARED + 1:
                            weigh(moe, SHARED)
                        weigh(moe, UP_AT[n])
                    if n == NORM_AT + 1 and following is not None:
                        norm_x(following)
                    need(pool, rden_done, r, n + 1)
                    pool.tensor_tensor(T1[sl][:, hs, :], T1[sl][:, hs, :], rden[sl][:, 1, hs].unsqueeze(2)
                                       .to_broadcast([P, 2, N + 1]), ALU.mult)
                    pool.tensor_tensor(T0[sl][:, hs, :], T0[sl][:, hs, :], rden[sl][:, 0, hs].unsqueeze(2)
                                       .to_broadcast([P, 2, P + 1]), ALU.mult).then_inc(norm_done.sem, 1)
                for t in range(TILES):
                    need(pool, y_var, r, t + 1)
                    pool.tensor_tensor(rstd2[:, t:t + 1], ve2[:, t:t + 1], neghalf[:, 0:1],
                                       ALU.pow).then_inc(rstd2_done.sem, 1)

            def weigh(m, k):
                e = ORDER[k]
                need(pool, h_done, m, k + 1)
                need(pool, wb_in[e % WB_RING], m, 16 * (e // WB_RING + 1))
                pool.tensor_tensor(H[:, k % H_RING, :], H[:, k % H_RING, :], Wb[:, e % WB_RING, :], ALU.mult) \
                    .then_inc(hw_done.sem, 1)

            norm_x(0)
            attention(0, None, 1)
            with pool.Fori(1, ROUNDS - 1) as r:
                attention(r, r - 1, r + 1)
            attention(ROUNDS - 1, ROUNDS - 2, None)
            for k in range(SHARED, BLOCKS):
                weigh(ROUNDS - 1, k)

        @block.scalar
        def _(act):
            act.wait_ge(ld_small.sem, PRE_SMALL)
            for c in range(KC):
                act.activation(Wkvn_in[:, c, 0:2 * DH], Wkvn_in[:, c, 0:2 * DH], ACT.Copy,
                               scale=gn[:, c:c + 1]).then_inc(w_scaled.sem, 1)
            act.wait_ge(ld_q.sem, 16)
            for c in range(KC):
                act.activation(Wq_in[:, c, :], Wq_in[:, c, :], ACT.Copy, scale=gn[:, c:c + 1]) \
                    .then_inc(w_scaled.sem, 1)
            act.wait_ge(pre_v.sem, V_SILU0)
            act.activation(pe, ph, ACT.Exp, scale=-1.0).then_inc(pre_a.sem, 1)
            act.wait_ge(ld_out.sem, 16)
            act.activation(Wout[0][:], Wout_in, ACT.Copy).then_inc(w_lead.sem, 1)
            act.wait_ge(w_scaled.sem, 2 * KC)
            act.activation(Wall[0][:, :, Q0:], Wq_in, ACT.Copy).then_inc(w_lead.sem, 1)
            for part in KB:
                act.activation(part[:].rearrange("p b h j -> p b (h j)"),
                               leaky[0][:].unsqueeze(1).to_broadcast([P, BB, 2 * N]), ACT.Copy) \
                    .then_inc(kb_zero.sem, 1)
            act.wait_ge(pre_v.sem, V_SILU1)
            act.activation(pe, ph, ACT.Exp, scale=-1.0).then_inc(pre_a.sem, 1)

            def keys(r):
                need(act, xnT_ps, r, 1)
                act.activation(xnT[0][:, 0, :], psT[:, 0, :], ACT.Copy).then_inc(xnT_a.sem, 1)
                for n in range(2):
                    need(act, kv_ps, r, n + 1)
                    act.activation(kvs[:, 2 * n:2 * n + 2, :],
                                   psT[:, n, :].rearrange("p (t c) -> p t c", t=2)[:, :, 0:KVN], ACT.Copy) \
                        .then_inc(kvs_done.sem, 1)

            def attention(r, moe, following):
                if moe is not None:
                    route(moe)
                for t in range(TILES):
                    if t >= 2 and moe is not None:
                        take_gate(moe, t - 2)
                    src = (psT if t % 2 == 0 else psS)[:, :, :].rearrange("p a c -> p (a c)")
                    need(act, q_ps, r, t + 1)
                    need(act, qss_done, r, t)
                    act.activation(sq, src, ACT.Square).then_inc(sq_done.sem, 1)
                    if t == 1 and moe is not None:
                        need(act, out_in, moe, 0)
                    act.activation(qs[t], src, ACT.Copy).then_inc(qs_done.sem, 1)
                    if t == 1:
                        if moe is not None:
                            softmax(moe)
                        need(act, kdT_ps, r, 1)
                        act.activation(KB[0][0:DH, :, 0, :], psO[0:DH, :].rearrange("p (b j) -> p b j", b=BB),
                                       ACT.Copy).then_inc(kb_a.sem, 1)
                for n in range(4):
                    turned_q(r, n)
                    if n == 1 and moe is not None:
                        take_gate(moe, 2)
                for n in range(ALL + VALUE_LAG):
                    for u in UNITS_AT.get(n, ()):
                        turned_q(r, u)
                    if n == 1 and moe is not None:
                        weights(moe)
                    if n >= VALUE_LAG:
                        head_out(r, n - VALUE_LAG)
                    if n < ALL:
                        exps(r, n // STEPS, n % STEPS)
                    if moe is not None and n in GATE_AT:
                        take_gate(moe, GATE_AT[n])
                    if moe is None and 0 <= n - 2 < BLOCKS:
                        e = n - 2
                        act.wait_ge(wraw_in[e % H_RING].sem, 16 * (e // H_RING + 1))
                        if e >= W_RING:
                            act.wait_ge(parts_out[e % W_RING].sem, 16 * (e // W_RING))
                        act.activation(Wgu[:, e % W_RING, 0], H[:, e % H_RING, :].rearrange(
                            "p (w c m) -> p w c m", w=2, c=KC), ACT.Copy).then_inc(lead_done.sem, 1)
                    if TURN_LAG <= n < ALL + TURN_LAG:
                        turned(r, n - TURN_LAG)
                if following is not None:
                    keys(following)

            def turned_q(r, n):
                t, half = n // 2, n % 2
                need(act, qT_ps, r, n + 1)
                act.activation(qT[0][:, 4 * half:4 * half + 4, t * P:(t + 1) * P],
                               q_bank(n).rearrange("p (q i) -> p q i", q=4), ACT.Copy).then_inc(qT_a.sem, 1)

            def head_out(r, n):
                g, s = n // STEPS, n % STEPS
                need(act, pv_ps, r, n + 1)
                act.activation(qT[0][:, STEPS * (g % 2) + s, (g // 2) * N:(g // 2 + 1) * N], psO[:, 0:N],
                               ACT.Copy).then_inc(o_lead.sem, 1)

            def exps(r, g, s):
                sl = g % 2
                n = g * STEPS + s
                need(act, s1_read, r, n + 1)
                for h in (2 * s, 2 * s + 1):
                    act.activation(T1[sl][:, h, :], T1[sl][:, h, :], ACT.Exp, scale=-1.0,
                                   bias=low[sl][:, 1, h:h + 1], accum_out=den[sl][:, 1, h:h + 1])
                need(act, s0_read, r, n + 1)
                for h in (2 * s, 2 * s + 1):
                    last = act.activation(T0[sl][:, h, :], T0[sl][:, h, :], ACT.Exp, scale=-1.0,
                                          bias=low[sl][:, 0, h:h + 1], accum_out=den[sl][:, 0, h:h + 1])
                last.then_inc(exp_done.sem, 1)

            def turned(r, n):
                need(act, pt1_ps, r, n + 1)
                need(act, pv_ps, r, n - 1)
                act.activation(PT[n % 2][:, :, P:3 * P], psT[:, 0, :].rearrange("p (h c) -> p h c", h=2),
                               ACT.Copy).then_inc(pt1_done.sem, 1)

            def route(m):
                need(act, x1T_ps, m, 1)
                act.activation(x1T[0][:, 0, :], psG[:], ACT.Copy).then_inc(x1T_a.sem, 1)

            def softmax(m):
                need(act, lg_done, m, 1)
                act.activation(lex[:], lgc[:], ACT.Exp, scale=0.5).then_inc(lex_done.sem, 1)

            def weights(m):
                need(act, wT_ps, m, 1)
                need(act, wscr_in, m - 1, 16)
                act.activation(WT[:], psO[0:E, :], ACT.Copy).then_inc(wT_done.sem, 1)

            def take_gate(m, k, alone=False):
                need(act, g_ps, m, k + 1)
                need(act, h_done, m, max(k - 1, 0))
                act.activation(leaky[k % 2][:], gate_bank(k, alone), ACT.Copy) \
                    .then_inc(gate_out.sem, 1)

            keys(0)
            attention(0, None, 1)
            with act.Fori(1, ROUNDS - 1) as r:
                attention(r, r - 1, r + 1)
            attention(ROUNDS - 1, ROUNDS - 2, None)
            route(ROUNDS - 1)
            softmax(ROUNDS - 1)
            weights(ROUNDS - 1)
            for k in range(BLOCKS):
                take_gate(ROUNDS - 1, k, True)

        @block.vector
        def _(dve):
            for ev in (leaky_done, h_done, ysum):
                dve.sem_inc(ev.sem, ev.base)
            count = [0]

            def pre(ins):
                count[0] += 1
                ins.then_inc(pre_v.sem, 1)
                dve.wait_ge(pre_v.sem, count[0])
                return count[0]

            for ap, v in ((leaky[0][:], 0.0), (MK[:], 0.0), (ones_bf[:], 1.0), (PNT[:], 0.0), (Unull[:], 0.0),
                          (relbuf, BIG), (ones64, 1.0), (vn_cols, 0.0)):
                pre(dve.memset(ap, v))
            dve.wait_ge(pre_p.sem, 5)
            pre(dve.tensor_copy(pos, posi[:]))
            pre(dve.tensor_copy(iota8[:], iota8i[:]))
            def norm_stats(r):
                ch = vchain["ln1"]
                ch.start(r)
                need(dve, xin_in, r, 16)
                for t in range(TILES):
                    ins = dve.bn_stats(stats[:, t, :], xin[:, t, :])
                ch.link(dve, ins)
                stand(dve, waited)
                for t in range(TILES):
                    ins = dve.bn_aggr(mv[:, t, :], stats[:, t, :])
                ch.link(dve, ins)
                ch.end()
                dve.tensor_scalar(ve[:], mv[:, :, 1], LN_EPS, None, ALU.add).then_inc(ln_var.sem, 1)

            def norm_x(r):
                need(dve, rstd_done, r, 1)
                for t in range(TILES):
                    dve.tensor_scalar(xin[:, t, :], xin[:, t, :], mv[:, t, 0:1], rstd[:, t:t + 1],
                                      ALU.subtract, ALU.mult).then_inc(xn_done.sem, 1)

            b2_b, nb_b, qs_b, ks_b, kn_b = (smalls_b[:, a:b] for a, b in
                                            ((0, 16), (16, 32), (32, 96), (96, 160), (160, 224)))

            def small_inputs():
                dve.wait_ge(ld_small.sem, PRE_SMALL)
                pre(dve.tensor_scalar(null_bias[:], nb_b, -1.0, None, ALU.mult))
                pre(dve.scalar_tensor_tensor(qk_scale[:], qs_b, -8.0, ks_b, ALU.mult, ALU.mult))
                for a in range(PAIRS // STEPS):
                    for i in range(2):
                        first = (STEPS * NULL_ROWS + 32) * a + i
                        pre(dve.tensor_copy(
                            vn_flat[i * DH:(i + 1) * DH,
                                    first:first + (STEPS - 1) * (NULL_ROWS + 2) + 1:NULL_ROWS + 2],
                            vnull[i * DH:(i + 1) * DH, 0:1].to_broadcast([DH, STEPS])))
                n = pre(dve.tensor_tensor(condx, condTs.unsqueeze(2).to_broadcast([COND, B, E]),
                                          wgTs.unsqueeze(1).to_broadcast([COND, B, E]), ALU.mult))
                assert n == V_CX, n
                pre(dve.tensor_tensor(ksq0, kn_b, kn_b, ALU.mult))
                pre(dve.tensor_reduce(knsq, ksq0, AX, ALU.add))
                n = pre(dve.tensor_scalar(nss, knsq, 1e-24, None, ALU.max))
                assert n == V_NSS, n

            def null_key():
                dve.wait_ge(pre_p.sem, 7)
                pre(dve.scalar_tensor_tensor(knull, kn_b, nrs, qk_scale[:], ALU.mult, ALU.mult))

            def null_columns():
                dve.wait_ge(w_scaled.sem, 2 * KC)
                for c in range(KC):
                    pre(dve.tensor_tensor(wprod, Wq_in[:, c, :].rearrange("p (h d) -> p h d", h=HEADS),
                                          knull.unsqueeze(1).to_broadcast([P, HEADS, DH]), ALU.mult))
                    pre(dve.tensor_reduce(wnull[:, c * HEADS:(c + 1) * HEADS], wprod, AX, ALU.add))
                pre(dve.tensor_copy(Wkvn_in[:, :, 2 * DH:], wnull.rearrange("p (c h) -> p c h", c=KC)))

            def kv_parts():
                for src, a, b in ((Wkvn_in, KV0, Q0), (Wt[:], 0, E)):
                    pre(dve.tensor_copy(Wall[0][:, :, a:b], src))
                    pre(dve.tensor_tensor(Wall[1][:, :, a:b], src, Wall[0][:, :, a:b].bitcast(F32),
                                          ALU.subtract))

            def others():
                dve.wait_ge(pre_t.sem, 3)
                pre(dve.tensor_copy(cond_logits[:].rearrange("p b e -> p (b e)"), psG[:, 0:B * E]))
                dve.wait_ge(pre_t.sem, 4)
                pre(dve.tensor_copy(Unull[0:NULL_ROWS, :], psY[0:NULL_ROWS, 0, 0:D]))

            dve.wait_ge(ld_rows.sem, 16)
            for t in range(2):
                pre(dve.scalar_tensor_tensor(ph[:, t, :], rows_b[:, 0, :], pos[:, t:t + 1], rows_b[:, 1, :],
                                             ALU.mult, ALU.add))
            for layer in range(2):
                for t in range(2):
                    pre(dve.bn_stats(pst[:, t, :], ph[:, t, :]))
                    pre(dve.bn_aggr(pmv[:, t, :], pst[:, t, :]))
                n = pre(dve.tensor_scalar(pve, pmv[:, :, 1], LN_EPS, None, ALU.add))
                assert n == (V_VAR0, V_VAR1)[layer], n
                if layer == 0:
                    small_inputs()
                dve.wait_ge(pre_p.sem, (6, 8)[layer])
                for t in range(2):
                    pre(dve.tensor_scalar(ph[:, t, :], ph[:, t, :], pmv[:, t, 0:1], prs[:, t:t + 1],
                                          ALU.subtract, ALU.mult))
                n = pre(dve.tensor_tensor(ph, ph, rows_b[:, 2 + 2 * layer, :].unsqueeze(1)
                                          .to_broadcast([P, 2, D]), ALU.mult))
                assert n == (V_SILU0, V_SILU1)[layer], n
                if layer == 0:
                    null_key()
                else:
                    norm_stats(0)
                dve.wait_ge(pre_a.sem, 1 + layer)
                pre(dve.tensor_scalar(pe, pe, 1.0, None, ALU.add))
                pre(dve.reciprocal(pe, pe))
                n = pre(dve.tensor_tensor(ph, ph, pe, ALU.mult))
                assert n == (V_ACT0, V_ACT1)[layer], n
                if layer == 1:
                    kv_parts()
                dve.wait_ge(pre_t.sem, (1, 5)[layer])
                n = pre(dve.tensor_copy(phT.rearrange("p c n -> p (c n)"), psS[:, layer, :]))
                assert n == (V_HT0, V_HT1)[layer], n
                if layer == 0:
                    null_columns()
                else:
                    others()
                    norm_x(0)
                dve.wait_ge(pre_t.sem, (2, 6)[layer])
                if layer == 0:
                    pre(dve.tensor_tensor(ph, psT[:, 0, :].rearrange("p (t d) -> p t d", t=2),
                                          rows_b[:, 3, :].unsqueeze(1).to_broadcast([P, 2, D]), ALU.add))
                else:
                    pre(dve.tensor_tensor(relb, psT[:, 1, 0:32].rearrange("p (t h) -> p t h", t=2),
                                          b2_b.unsqueeze(1).to_broadcast([P, 2, HEADS]), ALU.add))
                    n = pre(dve.tensor_scalar(relb, relb, -1.0, None, ALU.mult))
                    assert n == V_REL, n
            dve.wait_ge(pre_t.sem, 7)
            n = pre(dve.tensor_copy(relbuf[:, 0:N], psO[0:HEADS, 0:N]))
            assert n == V_RB == V_ALL, n
            dve.wait_ge(kb_zero.sem, 2)

            def keys(r):
                need(dve, xnT_ps, r, 2)
                dve.tensor_copy(xnT[0][:, 1, :], psT[:, 1, :]).then_inc(xnT_v.sem, 1)
                for c, ev in ((0, xnT_a), (1, xnT_v)):
                    need(dve, ev, r, 1)
                    dve.tensor_tensor(xnT[1][:, c, :], psT[:, c, :], xnT[0][:, c, :].bitcast(F32),
                                      ALU.subtract).then_inc(xnT_v.sem, 1)

            def attention(r, moe, following):
                ch = vchain["knorm"]
                ch.start(r)
                need(dve, kvs_done, r, 2)
                ch.link(dve, dve.tensor_tensor(ksq[:], kvs[:, :, 0:DH], kvs[:, :, 0:DH], ALU.mult))
                ch.link(dve, dve.tensor_reduce(kss[:], ksq[:], AX, ALU.add))
                dve.tensor_scalar(kss[:], kss[:], 1e-24, None, ALU.max).then_inc(kss_done.sem, 1)
                if moe is not None:
                    x1_parts(moe)
                sum_q(r, 0)
                need(dve, rk_done, r, 1)
                ch.link(dve, dve.tensor_tensor(kn[:], kvs[:, :, 0:DH], rk[:].unsqueeze(2)
                                               .to_broadcast([P, TILES, DH]), ALU.mult))
                ch.end()
                for i in range(2):
                    ins = dve.tensor_tensor(kd[:, :, i, :], kn[:], qk_scale[:].unsqueeze(1)
                                            .to_broadcast([P, TILES, DH]), ALU.mult)
                ins.then_inc(kd_done.sem, 1)
                need(dve, mask_in, r, 16)
                dve.tensor_scalar(MK[0:1, :], mask8[:], -BIG, BIG, ALU.mult, ALU.add).then_inc(mk_done.sem, 1)
                if moe is not None:
                    router_logits(moe)
                sum_q(r, 1)
                need(dve, kdT_ps, r, 1)
                kT = psO[:, :].rearrange("p (b j) -> p b j", b=BB)
                dve.tensor_copy(KB[0][DH:P, :, 1, :], kT[DH:P]).then_inc(kb_v.sem, 1)
                for i, ev in ((0, kb_a), (1, kb_v)):
                    need(dve, ev, r, 1)
                    rows_ = slice(i * DH, (i + 1) * DH)
                    dve.tensor_tensor(KB[1][rows_, :, i, :], kT[rows_], KB[0][rows_, :, i, :].bitcast(F32),
                                      ALU.subtract).then_inc(kb_v.sem, 1)
                if moe is not None:
                    leak(moe, 0)
                    hidden(moe, 0)
                sum_q(r, 2)
                if moe is not None:
                    router_best(moe)
                    leak(moe, 1)
                scale_q(dve, r, 1, qn_done)
                if moe is not None:
                    hidden(moe, 1)
                sum_q(r, 3)
                for n in range(4):
                    turned_q(r, n)
                    if n == 1 and moe is not None:
                        leak(moe, 2)
                        router_weights(moe)
                if moe is not None:
                    hidden(moe, 2)
                scale_q(dve, r, 2, qn_done)
                scale_q(dve, r, 3, qn_done)
                ch = vchain["null"]
                ch.start(r)
                null_parts(r, ch, 0)
                if moe is None:
                    dve.wait_ge(pre_d.sem, 48)
                for n in range(ALL + VALUE_LAG):
                    if n < ALL:
                        if n % STEPS == 0:
                            null_scores(r, n // STEPS)
                        scores(r, n // STEPS, n % STEPS)
                    if n >= VALUE_LAG:
                        head_out(r, n - VALUE_LAG)
                    for u in UNITS_AT.get(n, ()):
                        turned_q(r, u)
                    if moe is not None and n in GATE_AT:
                        leak(moe, GATE_AT[n])
                    if n == 3:
                        null_parts(r, ch, 1)
                        ch.end()
                    if moe is not None and n in UP_AT:
                        hidden(moe, UP_AT[n])
                    if moe is None and 0 <= n - 3 < BLOCKS:
                        e = n - 3
                        dve.wait_ge(lead_done.sem, e + 1)
                        dve.tensor_tensor(Wgu[:, e % W_RING, 1], H[:, e % H_RING, :].rearrange(
                            "p (w c m) -> p w c m", w=2, c=KC), Wgu[:, e % W_RING, 0].bitcast(F32),
                            ALU.subtract).then_inc(parts_done.sem, 1)
                    if 1 <= n <= ALL:
                        rdens(r, n - 1)
                    if following is not None:
                        if n == NORM_AT:
                            norm_stats(following)
                        if n == NORM_AT + 3:
                            norm_x(following)
                    if TURN_LAG <= n < ALL + TURN_LAG:
                        turned(r, n - TURN_LAG)
                        if (n - TURN_LAG) % STEPS == STEPS - 1:
                            null_turned(r, (n - TURN_LAG) // STEPS)
                if following is not None:
                    keys(following)
                need(dve, pt1_ps, r, ALL)
                need(dve, pt0_ps, r, ALL)
                if moe is not None:
                    for t in range(TILES):
                        sums(moe, t)
                    need(dve, ysum, moe, TILES)
                ch, cx = vchain["ln2"], vchain["x1"]
                ch.start(r)
                cx.start(r)
                for t, y in enumerate(wo_banks):
                    need(dve, wo_ps, r, t + 1)
                    ch.link(dve, dve.bn_stats(stats2[:, t, :], y))
                    stand(dve, waited)
                    ch.link(dve, dve.bn_aggr(mv2[:, t, :], stats2[:, t, :]))
                    dve.tensor_scalar(ve2[:, t:t + 1], mv2[:, t, 1:2], LN_EPS, None, ALU.add) \
                        .then_inc(y_var.sem, 1)
                    cx.link(dve, dve.scalar_tensor_tensor(x1[:, t, :], y, mv2[:, t, 0:1], gout[:],
                                                          ALU.subtract, ALU.mult))
                    need(dve, rstd2_done, r, t + 1)
                    if t == 0:
                        need(dve, xres_in, r, 16)
                    dve.scalar_tensor_tensor(x1[:, t, :], x1[:, t, :], rstd2[:, t:t + 1], xres[:, t, :],
                                             ALU.mult, ALU.add).then_inc(x1_done.sem, 1)
                ch.end()
                cx.end()

            def turned_q(r, n):
                t, half = n // 2, n % 2
                need(dve, qT_a, r, n + 1)
                cols = (slice(None), slice(4 * half, 4 * half + 4), slice(t * P, (t + 1) * P))
                dve.tensor_tensor(qT[1][cols], q_bank(n).rearrange("p (q i) -> p q i", q=4),
                                  qT[0][cols].bitcast(F32), ALU.subtract).then_inc(qT_v.sem, 1)

            def null_parts(r, ch, bb):
                ts = slice(2 * bb, 2 * bb + 2)
                ch.link(dve, dve.tensor_tensor(null_s[:, ts, :], kvs[:, ts, 2 * DH:], rq[:, ts, :], ALU.mult))
                ch.link(dve, dve.tensor_tensor(null_s[:, ts, :], null_s[:, ts, :], null_bias[:].unsqueeze(1)
                                               .to_broadcast([P, 2, HEADS]), ALU.add))

            def sum_q(r, t):
                need(dve, sq_done, r, t + 1)
                dve.tensor_reduce(qss[:, t, :], sq.rearrange("p (h d) -> p h d", h=HEADS), AX, ALU.add) \
                    .then_inc(qss_done.sem, 1)

            def rdens(r, n):
                need(dve, exp_done, r, n + 1)
                sl, hs = n // STEPS % 2, slice(2 * (n % STEPS), 2 * (n % STEPS) + 2)
                dve.reciprocal(rden[sl][:, :, hs], den[sl][:, :, hs]).then_inc(rden_done.sem, 1)

            def null_scores(r, g):
                sl, bb, h0 = g % 2, g // 2, GH * (g % 2)
                need(dve, pt1_ps, r, STEPS * (g - 1))
                need(dve, pt0_ps, r, STEPS * (g - 1))
                for tile, T, n in ((1, T1, N), (0, T0, P)):
                    dve.tensor_copy(T[sl][:, :, n:n + 1],
                                    null_s[:, 2 * bb + tile, h0:h0 + GH].unsqueeze(2))

            def scores(r, g, s):
                sl, bb, h0 = g % 2, g // 2, GH * (g % 2)
                n = g * STEPS + s + 1
                need(dve, s1_ps, r, n)
                stand(dve, waited)
                for i in range(2):
                    h = 2 * s + i
                    ins = dve.tensor_tensor_reduce(
                        T1[sl][:, h, 0:N], psS[:, 0, i * N:(i + 1) * N], bias[:, h0 + h, :], 1.0,
                        null_s[:, 2 * bb + 1, h0 + h:h0 + h + 1], ALU.add, ALU.min, low[sl][:, 1, h:h + 1])
                ins.then_inc(s1_read.sem, 1)
                need(dve, s0_ps, r, n)
                stand(dve, waited)
                for i in range(2):
                    h = 2 * s + i
                    ins = dve.tensor_tensor_reduce(
                        T0[sl][:, h, 0:P], psS[:, 1, i * P:(i + 1) * P], bias[:, h0 + h, P:N], 1.0,
                        null_s[:, 2 * bb, h0 + h:h0 + h + 1], ALU.add, ALU.min, low[sl][:, 0, h:h + 1])
                ins.then_inc(s0_read.sem, 1)

            def turned(r, n):
                need(dve, pt0_ps, r, n + 1)
                need(dve, pv_ps, r, n - 1)
                dve.tensor_copy(PT[n % 2][:, :, 0:P], psT[:, 1, 0:2 * P].rearrange("p (h c) -> p h c", h=2)) \
                    .then_inc(pt0_done.sem, 1)

            def null_turned(r, g):
                p0 = 32 * (g % 2)
                dve.tensor_copy(PNT[p0:p0 + GH, (g // 2) * N:(g // 2 + 1) * N], psT[0:GH, 1, 2 * P:4 * P]) \
                    .then_inc(pn_done.sem, 1)

            def head_out(r, n):
                g, s = n // STEPS, n % STEPS
                need(dve, o_lead, r, n + 1)
                cols = (slice(None), STEPS * (g % 2) + s, slice((g // 2) * N, (g // 2 + 1) * N))
                dve.tensor_tensor(qT[1][cols], psO[:, 0:N], qT[0][cols].bitcast(F32), ALU.subtract) \
                    .then_inc(o_done.sem, 1)

            def router_logits(m):
                ch = vchain["router"]
                ch.start(m)
                need(dve, lg_ps, m, 1)
                for i, bank in enumerate((psG, psO)):
                    ins = dve.tensor_tensor(
                        lg[:, 2 * i:2 * i + 2, :], bank[:, :].rearrange("p (t c) -> p t c", t=2)[:, :, 0:E],
                        cond_logits[:, bass.ds(m * BB + i, 1), :].to_broadcast([P, TILES // BB, E]), ALU.add)
                ch.link(dve, ins)
                ch.link(dve, dve.tensor_reduce(lgx[:], lg[:], AX, ALU.max))
                dve.tensor_tensor(lgc[:], lg[:], lgx[:].unsqueeze(2).to_broadcast([P, TILES, E]),
                                  ALU.subtract).then_inc(lg_done.sem, 1)

            def router_best(m):
                ch = vchain["router"]
                need(dve, lex_done, m, 1)
                ch.link(dve, dve.tensor_reduce(lsum[:], lex[:], AX, ALU.add))
                ch.link(dve, dve.reciprocal(lrec[:], lsum[:]))
                ch.link(dve, dve.tensor_tensor(score[:], lex[:], lrec[:].unsqueeze(2)
                                               .to_broadcast([P, TILES, E]), ALU.mult))
                stand(dve, waited)
                for t in range(TILES):
                    ins = dve.max(top[:, t, :], score[:, t, :])
                ch.link(dve, ins)
                stand(dve, waited)
                for t in range(TILES):
                    ins = dve.max_index(topi[:, t, :], top[:, t, :], score[:, t, :])
                ch.link(dve, ins)

            def router_weights(m):
                ch = vchain["router"]
                ch.link(dve, dve.tensor_copy(topf[:], topi[:, :, 0:2]))
                io = iota8[:].unsqueeze(1).to_broadcast([P, TILES, E])
                ch.link(dve, dve.tensor_tensor(oh1[:], io, topf[:, :, 0:1].to_broadcast([P, TILES, E]),
                                               ALU.is_equal))
                ch.link(dve, dve.tensor_tensor(oh2[:], io, topf[:, :, 1:2].to_broadcast([P, TILES, E]),
                                               ALU.is_equal))
                dve.tensor_tensor(tsum[:].unsqueeze(2), top[:, :, 0:1], top[:, :, 1:2], ALU.add)
                ch.link(dve, dve.tensor_tensor(oh1[:], oh1[:], oh2[:], ALU.add))
                ch.link(dve, dve.tensor_scalar(tsum[:], tsum[:], 1e-20, None, ALU.add))
                dve.reciprocal(trec[:], tsum[:])
                ch.link(dve, dve.tensor_tensor(wsel[:], oh1[:], score[:], ALU.mult))
                ch.link(dve, dve.tensor_tensor(oh2[:], wsel[:], trec[:].unsqueeze(2)
                                               .to_broadcast([P, TILES, E]), ALU.mult))
                ch.end()

            def x1_parts(m):
                need(dve, x1T_ps, m, 2)
                dve.tensor_copy(x1T[0][:, 1, :], psO[:]).then_inc(x1T_v.sem, 1)
                for c, bank, ev in ((0, psG, x1T_a), (1, psO, x1T_v)):
                    need(dve, ev, m, 1)
                    dve.tensor_tensor(x1T[1][:, c, :], bank[:], x1T[0][:, c, :].bitcast(F32),
                                      ALU.subtract).then_inc(x1T_v.sem, 1)

            def leak(m, k):
                need(dve, gate_out, m, k + 1)
                dve.scalar_tensor_tensor(leaky[k % 2][:], leaky[k % 2][:], LEAKY, leaky[k % 2][:],
                                         ALU.mult, ALU.max).then_inc(leaky_done.sem, 1)

            def hidden(m, k, alone=False):
                need(dve, u_ps, m, k + 1)
                need(dve, leaky_done, m, k + 1)
                if k >= H_RING:
                    need(dve, h_used, m, k + 1 - H_RING)
                dve.tensor_tensor(H[:, k % H_RING, :], up_bank(k, alone), leaky[k % 2][:], ALU.mult) \
                    .then_inc(h_done.sem, 1)

            def sums(m, t):
                need(dve, down_ps, m, t // 2 * 2 + 2)
                dve.tensor_tensor(yo[:, t, :], x1[:, t, :], psY[:, t // 2, (t % 2) * D:(t % 2 + 1) * D],
                                  ALU.add).then_inc(ysum.sem, 1)

            keys(0)
            attention(0, None, 1)
            with dve.Fori(1, ROUNDS - 1) as r:
                attention(r, r - 1, r + 1)
            attention(ROUNDS - 1, ROUNDS - 2, None)
            m = ROUNDS - 1
            x1_parts(m)
            router_logits(m)
            router_best(m)
            router_weights(m)
            for k in range(BLOCKS):
                leak(m, k)
                hidden(m, k, True)
            need(dve, out_in, m, 0)
            for t in range(TILES):
                sums(m, t)

        @block.tensor
        def _(te):
            te.sem_inc(u_ps.sem, u_ps.base)
            te.wait_ge(pre_p.sem, 5)
            for layer in range(2):
                te.wait_ge(pre_v.sem, (V_ACT0, V_ACT1)[layer])
                for t in range(2):
                    for c in range(KC):
                        mm = te.transpose(psS[:, layer, c * N + t * P:c * N + (t + 1) * P],
                                          ph[:, t, c * P:(c + 1) * P], ident[:])
                mm.then_inc(pre_t.sem, 1)
                te.wait_ge(pre_v.sem, (V_HT0, V_HT1)[layer])
                w, n = ((w1s, D), (w2s, HEADS))[layer]
                te.wait_ge(ld_small.sem, PRE_SMALL)
                for t in range(2):
                    for c in range(KC):
                        mm = te.matmul(psT[:, layer, t * n:(t + 1) * n], phT[:, c, t * P:(t + 1) * P],
                                       w[:, c, :], start=(c == 0), stop=(c == KC - 1))
                mm.then_inc(pre_t.sem, 1)
                if layer == 0:
                    te.wait_ge(pre_v.sem, V_CX)
                    te.matmul(psG[:, 0:B * E], ones64, condx.rearrange("p b e -> p (b e)"), start=True,
                              stop=True).then_inc(pre_t.sem, 1)
                    te.wait_ge(ld_out.sem, 16)
                    for p in range(PAIRS):
                        mm = te.matmul(psY[0:NULL_ROWS, 0, 0:D], vn_cols[:, p, :], Wout_in[:, p, :],
                                       start=(p == 0), stop=(p == PAIRS - 1))
                    mm.then_inc(pre_t.sem, 1)
            te.wait_ge(pre_v.sem, V_REL)
            for t in range(2):
                mm = te.transpose(psO[0:HEADS, t * P:(t + 1) * P], relb[:, t, :], ident[:])
            mm.then_inc(pre_t.sem, 1)

            def turn_x(r):
                need(te, xn_done, r, TILES)
                for c in range(KC):
                    for t in range(TILES):
                        mm = te.transpose(psT[:, c, t * P:(t + 1) * P], xin[:, t, c * P:(c + 1) * P], ident[:])
                    mm.then_inc(xnT_ps.sem, 1)

            def keys(r):
                need(te, xnT_a, r, 1)
                need(te, xnT_v, r, 3)
                for t in range(TILES):
                    for c in range(KC):
                        mm = products(te, psT[:, t // 2, (t % 2) * 2 * P:(t % 2 + 1) * 2 * P],
                                      [part[:, c, t * P:(t + 1) * P] for part in xnT],
                                      [part[:, c, KV0:KV0 + 2 * P] for part in Wall], c == 0, c == KC - 1)
                    if t % 2 == 1:
                        mm.then_inc(kv_ps.sem, 1)

            def q_half(t, half):
                bank = psT if t % 2 == 0 else psS
                for c in range(KC):
                    mm = products(te, bank[:, half, :], [part[:, c, t * P:(t + 1) * P] for part in xnT],
                                  [part[:, c, Q0 + half * 512:Q0 + (half + 1) * 512] for part in Wall],
                                  c == 0, c == KC - 1)
                return mm

            def q_first(r):
                need(te, kvs_done, r, 2)
                q_half(0, 0)
                q_half(0, 1).then_inc(q_ps.sem, 1)

            def turn_q(r, n):
                t, half = n // 2, n % 2
                if t < POOL_TILES:
                    need(te, qn_pool, r, t + 1)
                else:
                    need(te, qn_done, r, t + 1 - POOL_TILES)
                if n < 4:
                    need(te, qs_done, r, 3 + n // 2)
                else:
                    need(te, qT_v, r, n - 3 if n < 6 else n - 1)
                for q in range(4):
                    mm = te.transpose(q_bank(n)[:, q * P:(q + 1) * P],
                                      qs[t][:, (4 * half + q) * P:(4 * half + q + 1) * P], ident[:])
                mm.then_inc(qT_ps.sem, 1)

            def attention(r, moe, following):
                need(te, x1_done, r - 1, TILES)
                if moe is not None:
                    turn_x1(moe)
                q_half(1, 0)
                q_half(1, 1).then_inc(q_ps.sem, 1)
                if moe is not None:
                    logits(moe)
                need(te, qs_done, r, 1)
                q_half(2, 0)
                need(te, kd_done, r, 1)
                if moe is not None:
                    te.wait_ge(vchain["router"].ev.sem, vchain["router"].ev.at(moe, 1))
                for tt in range(TILES):
                    mm = te.transpose(psO[:, tt * P:(tt + 1) * P],
                                      kd[:, tt, :, :].rearrange("p a d -> p (a d)"), ident[:])
                mm.then_inc(kdT_ps.sem, 1)
                if moe is not None:
                    gate(moe, 0)
                q_half(2, 1).then_inc(q_ps.sem, 1)
                if moe is not None:
                    up(moe, 0)
                need(te, qs_done, r, 2)
                q_half(3, 0)
                if moe is not None:
                    gate(moe, 1)
                q_half(3, 1).then_inc(q_ps.sem, 1)
                need(te, kb_a, r, 1)
                need(te, kb_v, r, 3)
                if moe is not None:
                    up(moe, 1)
                for n in range(4):
                    turn_q(r, n)
                    if n == 1 and moe is not None:
                        gate(moe, 2)
                if moe is not None:
                    up(moe, 2)
                    down(moe, 0)
                need(te, mk_done, r, 1)
                for n in range(ALL + VALUE_LAG):
                    if n == 0:
                        need(te, qT_a, r, 4)
                        need(te, qT_v, r, 4)
                    if n < ALL:
                        score(r, n // STEPS, n % STEPS)
                    if n == VALUE_LAG and moe is not None:
                        need(te, wT_done, moe, 1)
                    if n >= VALUE_LAG:
                        value(r, n - VALUE_LAG)
                    for u in UNITS_AT.get(n, ()):
                        turn_q(r, u)
                    if moe is not None:
                        if n == 0:
                            turn_weights(moe)
                        if n in DOWN_AT:
                            down(moe, DOWN_AT[n])
                        if n in GATE_AT:
                            gate(moe, GATE_AT[n])
                        if n in UP_AT:
                            up(moe, UP_AT[n])
                    if n == TURN_LAG:
                        need(te, qT_a, r, 2 * TILES)
                        need(te, qT_v, r, 2 * TILES)
                    if TURN_LAG <= n < ALL + TURN_LAG:
                        turn(r, n - TURN_LAG)
                if following is not None:
                    turn_x(following)
                need(te, o_done, r, ALL)
                need(te, pn_done, r, GROUPS)
                need(te, s1_read, r, ALL)
                need(te, s0_read, r, ALL)
                for t in range(TILES):
                    if t == 2 and following is not None:
                        keys(following)
                    if t == 2 and moe is not None:
                        need(te, h_done, moe, BLOCKS)
                    dst = wo_banks[t]
                    for p in range(PAIRS):
                        products(te, dst, [part[:, p, t * P:(t + 1) * P] for part in qT],
                                 [part[:, p, :] for part in Wout], p == 0, False)
                    te.matmul(dst, PNT[:, t * P:(t + 1) * P], Unull[:], start=False, stop=True) \
                        .then_inc(wo_ps.sem, 1)
                if following is not None:
                    q_first(following)

            def score(r, g, s):
                bb, p = g // 2, STEPS * (g % 2) + s
                n = g * STEPS + s
                q0 = bb * N
                need(te, s1_read, r, n)
                products(te, psS[:, 0, :], [part[:, p, q0 + P:q0 + N] for part in qT],
                         [part[:, bb, :, :].rearrange("p h j -> p (h j)") for part in KB], True, False)
                te.matmul(psS[:, 0, :], ones_bf[:], MK[:, q0:q0 + N].unsqueeze(1).to_broadcast([P, 2, N]),
                          start=False, stop=True).then_inc(s1_ps.sem, 1)
                need(te, s0_read, r, n)
                products(te, psS[:, 1, 0:2 * P], [part[:, p, q0:q0 + P] for part in qT],
                         [part[:, bb, :, 0:P] for part in KB], True, False)
                te.matmul(psS[:, 1, 0:2 * P], ones_bf[:], MK[:, q0:q0 + P].unsqueeze(1).to_broadcast([P, 2, P]),
                          start=False, stop=True).then_inc(s0_ps.sem, 1)

            def turn(r, n):
                g, s = n // STEPS, n % STEPS
                sl = g % 2
                need(te, norm_done, r, n + 1)
                need(te, pt1_done, r, n)
                for i in range(2):
                    for j in range(2):
                        mm = te.transpose(psT[:, 0, (2 * i + j) * P:(2 * i + j + 1) * P],
                                          T1[sl][:, 2 * s + i, j * P:(j + 1) * P], ident[:])
                mm.then_inc(pt1_ps.sem, 1)
                need(te, pt0_done, r, n)
                if s == 0:
                    need(te, pn_done, r, g)
                for i in range(2):
                    mm = te.transpose(psT[:, 1, i * P:(i + 1) * P], T0[sl][:, 2 * s + i, 0:P], ident[:])
                if s == STEPS - 1:
                    te.transpose(psT[0:GH, 1, 2 * P:3 * P], T0[sl][:, :, P], ident[:])
                    mm = te.transpose(psT[0:GH, 1, 3 * P:4 * P], T1[sl][:, :, N], ident[:])
                mm.then_inc(pt0_ps.sem, 1)

            def value(r, n):
                bb = n // STEPS // 2
                need(te, pt1_done, r, n + 1)
                need(te, pt0_done, r, n + 1)
                need(te, o_done, r, n)
                for i in range(2):
                    te.matmul(psO[i * DH:(i + 1) * DH, 0:N], kvs[:, 2 * bb, DH:2 * DH], PT[n % 2][:, i, 0:N],
                              start=True, stop=False)
                for i in range(2):
                    mm = te.matmul(psO[i * DH:(i + 1) * DH, P:N], kvs[:, 2 * bb + 1, DH:2 * DH],
                                   PT[n % 2][:, i, N:N + P], start=False, stop=True)
                mm.then_inc(pv_ps.sem, 1)

            def turn_x1(m):
                need(te, x1_done, m, TILES)
                need(te, ysum, m - 1, TILES)
                for c, bank in ((0, psG), (1, psO)):
                    for t in range(TILES):
                        mm = te.transpose(bank[:, t * P:(t + 1) * P], x1[:, t, c * P:(c + 1) * P], ident[:])
                    mm.then_inc(x1T_ps.sem, 1)

            def logits(m):
                need(te, x1T_v, m, 3)
                for t in range(TILES):
                    for c in range(KC):
                        mm = products(te, (psG, psO)[t // 2][:, (t % 2) * 2 * P:(t % 2 + 1) * 2 * P],
                                      [part[:, c, t * P:(t + 1) * P] for part in x1T],
                                      [part[:, c, 0:2 * P] for part in Wall], c == 0, c == KC - 1)
                mm.then_inc(lg_ps.sem, 1)

            def turn_weights(m):
                te.wait_ge(vchain["router"].ev.sem, vchain["router"].ev.at(m, vchain["router"].ev.per))
                for t in range(TILES):
                    mm = te.transpose(psO[0:E, t * P:(t + 1) * P], oh2[:, t, :], ident[:])
                mm.then_inc(wT_ps.sem, 1)

            def gate_up(m, k, w, bank):
                for c in range(KC):
                    mm = products(te, bank, [Wgu[:, k % W_RING, part, w, c, :] for part in range(2)],
                                  [part[:, c, :] for part in x1T], c == 0, c == KC - 1)
                return mm

            def gate(m, k, alone=False):
                need(te, wgu_ld[k % W_RING], m, 16 * (k // W_RING + 1))
                if alone:
                    need(te, gate_out, m, k - 1)
                else:
                    if k == 0:
                        te.wait_ge(vchain["router"].ev.sem, vchain["router"].ev.at(m, 1))
                    need(te, h_done, m, k)
                gate_up(m, k, 0, gate_bank(k, alone)).then_inc(g_ps.sem, 1)

            def up(m, k, alone=False):
                if alone:
                    need(te, h_done, m, k - 1)
                else:
                    need(te, gate_out, m, k + 1)
                gate_up(m, k, 1, up_bank(k, alone)).then_inc(u_ps.sem, 1)

            def down(m, k):
                if k < SHARED:
                    need(te, h_done, m, k + 1)
                else:
                    need(te, hw_done, m, k + 1 - SHARED)
                if k == 0:
                    need(te, ysum, m - 1, TILES)
                for t in range(TILES):
                    mm = te.matmul(psY[:, t // 2, (t % 2) * D:(t % 2 + 1) * D],
                                   H[:, k % H_RING, t * P:(t + 1) * P], Wd[:, ORDER[k], :],
                                   start=(k == 0 and t % 2 == 0), stop=(k == BLOCKS - 1), skip_group_check=True)
                    if k == BLOCKS - 1:
                        mm.then_inc(down_ps.sem, 1)
                if k < BLOCKS - 1:
                    mm.then_inc(h_used.sem, 1)

            turn_x(0)
            te.wait_ge(pre_v.sem, V_ALL)
            te.wait_ge(w_trail.sem, 2)
            te.wait_ge(ld_down.sem, 16)
            keys(0)
            q_first(0)
            attention(0, None, 1)
            with te.Fori(1, ROUNDS - 1) as r:
                attention(r, r - 1, r + 1)
            attention(ROUNDS - 1, ROUNDS - 2, None)
            m = ROUNDS - 1
            turn_x1(m)
            logits(m)
            for k in range(BLOCKS):
                if k == 2:
                    turn_weights(m)
                gate(m, k, True)
                up(m, k, True)
                if k >= 2:
                    down(m, k - 2)
            down(m, BLOCKS - 2)
            down(m, BLOCKS - 1)


def kernel(**a):
    import concourse.bacc as bacc
    from concourse.bass_utils import run_bass_kernel_spmd

    a = {k: np.asarray(v) for k, v in a.items()}

    def chunks(w):
        return w.reshape(-1, P, w.shape[-1]).transpose(1, 0, 2)

    def blocks(w, shared):
        both = np.concatenate([w, shared.reshape(D, SHARED, P).transpose(1, 0, 2)])
        return both.reshape(BLOCKS, KC, P, P).transpose(0, 2, 1, 3)

    cond = a["cond_64"]
    arrays = {
        "x": a["x"].reshape(B * N, D),
        "condT": cond.T,
        "condR": cond,
        "mask": a["mask_BxS_bf1"].reshape(1, B * N).view(np.uint8),
        "wq": chunks(a["L0_cond_Wq"]),
        "wkv": chunks(a["L0_cond_Wkv"]),
        "wout": chunks(a["L0_cond_Wout"]),
        "wgu": np.stack([blocks(a["L1_cond_w_gate"], a["L1_cond_sw_gate"]),
                         blocks(a["L1_cond_w_up"], a["L1_cond_sw_up"])], 2),
        "wdown": np.concatenate([a["L1_cond_w_down"], a["L1_cond_sw_down"].reshape(SHARED, P, D)]).transpose(1, 0, 2),
        "wt": chunks(a["L1_cond_wt"].T),
        "wgT": a["L1_cond_wg"].T,
        "gnorm": a["L0_cond_g_norm"].reshape(KC, P).T,
        "rows": np.stack([a["L0_cond_w0"][0], a["L0_cond_b0"], a["L0_cond_g0"], a["L0_cond_b1"],
                          a["L0_cond_g1"], a["L0_cond_g_out"]]),
        "smalls": np.concatenate([a["L0_cond_b2"], a["L0_cond_null_attn_bias"], a["L0_cond_q_scale"],
                                  a["L0_cond_k_scale"], cond[0]]).reshape(1, -1),
        "w1": chunks(a["L0_cond_w1"]),
        "w2": chunks(a["L0_cond_w2"]),
    }
    nc = bacc.Bacc("TRN2", target_bir_lowering=False, num_devices=1)
    feeds, args = {}, []
    for name, v in arrays.items():
        v = np.ascontiguousarray(v)
        feeds["in_" + name] = v
        args.append(nc.dram_tensor("in_" + name, v.shape, mybir.dt.from_np(v.dtype), kind="ExternalInput").ap())
    out = nc.dram_tensor("out", (B * N, D), F32, kind="ExternalOutput").ap()
    attention_moe(nc, *args, out)
    r = run_bass_kernel_spmd(nc, [feeds], core_ids=[0])
    return r.results[0]["out"].reshape(B, N, D)
```
